# Optimizing a Trainium2 kernel written in Bass

```python
import numpy as np
import jax
import jax.numpy as jnp

def _softmax(x, axis=-1):
    return jax.nn.softmax(x, axis=axis)

def _gelu(x):
    return jax.nn.gelu(x, approximate=True)

def _silu(x):
    return jax.nn.silu(x)

def _sigmoid(x):
    return jax.nn.sigmoid(x)

def _layernorm(x, axis=-1, eps=1e-05):
    m = jnp.mean(x, axis=axis, keepdims=True)
    v = jnp.var(x, axis=axis, keepdims=True)
    return (x - m) / jnp.sqrt(v + eps)

def _scatter_add(tgt, idx, src, axis=0):
    return tgt.at[idx].add(src)

def _segment_sum(src, seg, n):
    return jax.ops.segment_sum(src, seg, n)
kernel_name = 'mk_xattn_seq_d1_seqx_r4_bfd49b'

def setup_inputs(seed: int=0):
    np.random.seed(seed)
    _w = jnp.asarray

    def _rec_inputs():
        import jax
        import jax.numpy as jnp
        _rk = jax.random.key(seed)
        x = 7.22e-05 + 1 * jax.random.normal(jax.random.fold_in(_rk, 1), (32, 256, 256), jnp.float32)
        _lenS = 256 - jax.random.randint(jax.random.fold_in(_rk, 7), (32,), 0, max(1, 256 // 4) + 1, jnp.int32)
        _lenS2 = 256 - jax.random.randint(jax.random.fold_in(_rk, 8), (32,), 0, max(1, 256 // 4) + 1, jnp.int32)
        _ctx_1024P = jax.random.normal(jax.random.fold_in(_rk, 11), (32, 16, 256), jnp.float32)
        _ctx_1024c = jax.random.dirichlet(jax.random.fold_in(_rk, 511), 0.3 * jnp.ones((16,), jnp.float32), (32, 256))
        _ctx_1024t = jnp.einsum('bsk,bkd->bsd', _ctx_1024c, _ctx_1024P)
        _ctx_1024t = _ctx_1024t * jax.lax.rsqrt(jnp.mean(jnp.square(_ctx_1024t)) + 1e-12) * 0.953939
        ctx_1024 = 4.13588e-05 + 0.999923 * (_ctx_1024t + 0.3 * jax.random.normal(jax.random.fold_in(_rk, 611), (32, 256, 256), jnp.float32))
        itok_BxS2_4_31999 = jax.random.randint(jax.random.fold_in(_rk, 12), (32, 256), 4, 8000, jnp.int32)
        _ctxb_2048x64P = jax.random.normal(jax.random.fold_in(_rk, 13), (32, 16, 64), jnp.float32)
        _ctxb_2048x64c = jax.random.dirichlet(jax.random.fold_in(_rk, 513), 0.3 * jnp.ones((16,), jnp.float32), (32, 256))
        _ctxb_2048x64t = jnp.einsum('bsk,bkd->bsd', _ctxb_2048x64c, _ctxb_2048x64P)
        _ctxb_2048x64t = _ctxb_2048x64t * jax.lax.rsqrt(jnp.mean(jnp.square(_ctxb_2048x64t)) + 1e-12) * 0.953939
        ctxb_2048x64 = 0.50053 + 0.288505 * (_ctxb_2048x64t + 0.3 * jax.random.normal(jax.random.fold_in(_rk, 613), (32, 256, 64), jnp.float32))
        return (x, ctx_1024, itok_BxS2_4_31999, ctxb_2048x64)
    x, ctx_1024, itok_BxS2_4_31999, ctxb_2048x64 = _rec_inputs()

    def _L0_xattn_setup():
        import jax, jax.numpy as jnp
        import numpy as np
        BATCH, T, H, S, P, NH = (4, 512, 256, 64, 64, 8)
        HD = H // NH

        def _layernorm(x, g, b):
            mu = jnp.mean(x, axis=-1, keepdims=True)
            var = jnp.mean((x - mu) ** 2, axis=-1, keepdims=True)
            return (x - mu) * jax.lax.rsqrt(var + 1e-05) * g + b

        def _mha(q_in, kv_in, W_qkv, b_qkv, W_o, b_o):
            Wq, Wk, Wv = jnp.split(W_qkv, 3, axis=0)
            bq, bk, bv = jnp.split(b_qkv, 3, axis=0)

            def heads(x, W, b):
                y = x @ W.T + b
                return y.reshape(y.shape[0], y.shape[1], NH, HD).transpose(0, 2, 1, 3)
            q, k, v = (heads(q_in, Wq, bq), heads(kv_in, Wk, bk), heads(kv_in, Wv, bv))
            scores = jnp.einsum('bhqd,bhkd->bhqk', q, k) * (1.0 / np.sqrt(HD))
            attn = jax.nn.softmax(scores, axis=-1)
            out = jnp.einsum('bhqk,bhkd->bhqd', attn, v)
            out = out.transpose(0, 2, 1, 3).reshape(q_in.shape)
            return out @ W_o.T + b_o
        key = jax.random.key(seed)
        ks = jax.random.split(key, 16)
        sH = 1.0 / np.sqrt(H)
        d = {}
        d['builder_state'] = jax.random.normal(ks[0], (BATCH, T, H), jnp.float32)
        d['base_state'] = jax.random.normal(ks[1], (BATCH, T, H), jnp.float32)
        d['input_ids'] = jax.random.randint(ks[2], (BATCH, T), 0, 8000)
        d['program_probs'] = jax.random.uniform(ks[3], (BATCH, T, P), jnp.float32)
        d['A'] = jax.random.normal(ks[4], (S, S), jnp.float32) * (0.5 / np.sqrt(S))
        d['Bmat'] = jax.random.normal(ks[5], (H, S), jnp.float32) * sH
        d['Cmat'] = jax.random.normal(ks[6], (S, H), jnp.float32) * (1.0 / np.sqrt(S))
        d['W_in'] = jax.random.normal(ks[7], (H, H), jnp.float32) * sH
        d['b_in'] = jnp.zeros((H,), jnp.float32)
        d['W_qkv'] = jax.random.normal(ks[8], (3 * H, H), jnp.float32) * sH
        d['b_qkv'] = jnp.zeros((3 * H,), jnp.float32)
        d['W_o'] = jax.random.normal(ks[9], (H, H), jnp.float32) * sH
        d['b_o'] = jnp.zeros((H,), jnp.float32)
        d['W_prog'] = jax.random.normal(ks[10], (H, P), jnp.float32) * (1.0 / np.sqrt(P))
        d['b_prog'] = jnp.zeros((H,), jnp.float32)
        d['g1'] = jnp.ones((H,), jnp.float32)
        d['beta1'] = jnp.zeros((H,), jnp.float32)
        d['g2'] = jnp.ones((H,), jnp.float32)
        d['beta2'] = jnp.zeros((H,), jnp.float32)
        return d
    _L0_xattn_all = _L0_xattn_setup()
    _L0_xattn_in = {k: v for k, v in _L0_xattn_all.items() if k in ('A', 'Bmat', 'Cmat', 'W_in', 'b_in', 'W_qkv', 'b_qkv', 'W_o', 'b_o', 'W_prog', 'b_prog', 'g1', 'beta1', 'g2', 'beta2')}
    del _L0_xattn_all
    return {'x': x, 'ctx_1024': ctx_1024, 'itok_BxS2_4_31999': itok_BxS2_4_31999, 'ctxb_2048x64': ctxb_2048x64, 'L0_xattn_A': _L0_xattn_in['A'], 'L0_xattn_Bmat': _L0_xattn_in['Bmat'], 'L0_xattn_Cmat': _L0_xattn_in['Cmat'], 'L0_xattn_W_in': _L0_xattn_in['W_in'], 'L0_xattn_b_in': _L0_xattn_in['b_in'], 'L0_xattn_W_qkv': _L0_xattn_in['W_qkv'], 'L0_xattn_b_qkv': _L0_xattn_in['b_qkv'], 'L0_xattn_W_o': _L0_xattn_in['W_o'], 'L0_xattn_b_o': _L0_xattn_in['b_o'], 'L0_xattn_W_prog': _L0_xattn_in['W_prog'], 'L0_xattn_b_prog': _L0_xattn_in['b_prog'], 'L0_xattn_g1': _L0_xattn_in['g1'], 'L0_xattn_beta1': _L0_xattn_in['beta1'], 'L0_xattn_g2': _L0_xattn_in['g2'], 'L0_xattn_beta2': _L0_xattn_in['beta2']}

def reference(x, ctx_1024, itok_BxS2_4_31999, ctxb_2048x64, L0_xattn_A, L0_xattn_Bmat, L0_xattn_Cmat, L0_xattn_W_in, L0_xattn_b_in, L0_xattn_W_qkv, L0_xattn_b_qkv, L0_xattn_W_o, L0_xattn_b_o, L0_xattn_W_prog, L0_xattn_b_prog, L0_xattn_g1, L0_xattn_beta1, L0_xattn_g2, L0_xattn_beta2):
    import jax
    import jax.numpy as jnp

    def _L0_xattn_ref(builder_state, base_state, input_ids, program_probs, A, Bmat, Cmat, W_in, b_in, W_qkv, b_qkv, W_o, b_o, W_prog, b_prog, g1, beta1, g2, beta2):
        import jax, jax.numpy as jnp
        import numpy as np
        BATCH, T, H, S, P, NH = (4, 512, 256, 64, 64, 8)
        HD = H // NH

        def _layernorm(x, g, b):
            mu = jnp.mean(x, axis=-1, keepdims=True)
            var = jnp.mean((x - mu) ** 2, axis=-1, keepdims=True)
            return (x - mu) * jax.lax.rsqrt(var + 1e-05) * g + b

        def _mha(q_in, kv_in, W_qkv, b_qkv, W_o, b_o):
            Wq, Wk, Wv = jnp.split(W_qkv, 3, axis=0)
            bq, bk, bv = jnp.split(b_qkv, 3, axis=0)

            def heads(x, W, b):
                y = x @ W.T + b
                return y.reshape(y.shape[0], y.shape[1], NH, HD).transpose(0, 2, 1, 3)
            q, k, v = (heads(q_in, Wq, bq), heads(kv_in, Wk, bk), heads(kv_in, Wv, bv))
            scores = jnp.einsum('bhqd,bhkd->bhqk', q, k) * (1.0 / np.sqrt(HD))
            attn = jax.nn.softmax(scores, axis=-1)
            out = jnp.einsum('bhqk,bhkd->bhqd', attn, v)
            out = out.transpose(0, 2, 1, 3).reshape(q_in.shape)
            return out @ W_o.T + b_o
        residual = builder_state
        x = _layernorm(builder_state, g1, beta1)
        base_n = _layernorm(base_state, g1, beta1)
        x = residual + _mha(x, base_n, W_qkv, b_qkv, W_o, b_o)
        residual = x
        xn = _layernorm(x, g2, beta2)
        U = (xn @ W_in.T + b_in) @ Bmat

        def step(s, u_t):
            s = jax.nn.silu(s @ A.T) + u_t
            return (s, s)
        _, states = jax.lax.scan(step, jnp.zeros((builder_state.shape[0], S), U.dtype), U.transpose(1, 0, 2))
        ssm_out = jnp.einsum('tbs,sh->bth', states, Cmat)
        x = residual + ssm_out
        mod = program_probs.mean(axis=1) @ W_prog.T + b_prog
        return x + mod[:, None, :]
    x = _L0_xattn_ref(x, ctx_1024, itok_BxS2_4_31999, ctxb_2048x64, L0_xattn_A, L0_xattn_Bmat, L0_xattn_Cmat, L0_xattn_W_in, L0_xattn_b_in, L0_xattn_W_qkv, L0_xattn_b_qkv, L0_xattn_W_o, L0_xattn_b_o, L0_xattn_W_prog, L0_xattn_b_prog, L0_xattn_g1, L0_xattn_beta1, L0_xattn_g2, L0_xattn_beta2)
    return x

_drawn_inputs = setup_inputs


def setup_inputs(seed=0):
    import zlib

    import numpy as np

    out = dict(_drawn_inputs(seed))
    spreads = {'L0_xattn_b_in': (0.0, 0.1),
     'L0_xattn_b_qkv': (0.0, 0.1),
     'L0_xattn_b_o': (0.0, 0.1),
     'L0_xattn_b_prog': (0.0, 0.1),
     'L0_xattn_g1': (1.0, 0.2),
     'L0_xattn_beta1': (0.0, 0.1),
     'L0_xattn_g2': (1.0, 0.2),
     'L0_xattn_beta2': (0.0, 0.1)}
    factors = {}
    for name, (base, spread) in spreads.items():
        noise = np.random.default_rng([zlib.crc32(name.encode()), seed]).standard_normal(out[name].shape)
        drawn = base * np.exp(spread * noise) if base else spread * noise
        out[name] = jnp.asarray(drawn.astype(out[name].dtype))
    for name, factor in factors.items():
        out[name] = (out[name] * factor).astype(out[name].dtype)
    return out
```

```python
from contextlib import ExitStack

import concourse.bass as bass
from concourse import mybir

F32 = mybir.dt.float32
F32R = mybir.dt.float32r
ALU = mybir.AluOpType
ACT = mybir.ActivationFunctionType
AX = mybir.AxisListType

P = 128
EPS = 1e-5


def xattn_seq_kernel(nc, x, ctx_in, itok, probs, A, Bmat, Cmat, W_in, b_in, W_qkv, b_qkv, W_o, b_o,
                     W_prog, b_prog, g1, beta1, g2, beta2, out):
    B, T, H = x.shape
    S = A.shape[0]
    PR = probs.shape[2]
    HD = 32
    NH = H // HD
    NG = H // P
    NJ = P // HD
    NC = T // P
    SCALE = float(HD) ** -0.5
    TQ = P // B
    SCAN_UNROLL = 15
    assert (T - 1) % SCAN_UNROLL == 0 and 2 * S == P

    stack = ExitStack()
    with stack:
        def sb(name, shape, dt=F32):
            return stack.enter_context(nc.sbuf_tensor(name, shape, dt))

        def sem(name):
            return stack.enter_context(nc.semaphore(name))

        def sem2(name):
            return [sem(f"{name}{i}") for i in range(2)]

        ident = sb("ident", [P, P])
        sel_head = sb("sel_head", [P, NH], F32R)
        ones_hd = sb("ones_hd", [P, HD])
        minus_half = sb("minus_half", [P, 4])
        wT = sb("wT", [P, NG, 3 * H])
        woT = sb("woT", [P, NG, H])
        wu_raw = sb("wu_raw", [P, NG, S])
        wu = sb("wu", [P, NG, S])
        aT2 = sb("aT2", [P, S])
        c2 = sb("c2", [P, H])
        wprogT = sb("wprogT", [PR, H])
        vecs = sb("vecs", [P, 5, NG])
        bqk_perm = sb("bqk_perm", [P, 4])
        bv_nat = sb("bv_nat", [P, NG])
        bqk = sb("bqk", [P, 4])
        bv = sb("bv", [P, NG])
        bu = sb("bu", [P, 1])
        bo = sb("bo", [P, H])
        sel_batch = sb("sel_batch", [P, B])
        prob_part = sb("prob_part", [P, PR])
        prob_meanT = sb("prob_meanT", [PR, B])
        mod_rows = sb("mod_rows", [B, H])

        x_in = sb("x_in", [P, 2, NC, H])
        c_in = sb("c_in", [P, 2, NC, H])
        stat1 = sb("stat1", [P, 4, 6])
        mv1 = sb("mv1", [P, 2, 4, 2])
        nmean1 = sb("nmean1", [P, 2, 4])
        rstd1 = sb("rstd1", [P, 2, 4])
        xn = sb("xn", [P, 2, NC, H])
        cn = sb("cn", [P, 2, NC, H])
        xnT = sb("xnT", [P, NG, T])
        cnT = sb("cnT", [P, NG, T])
        qk32 = sb("qk32", [P, 2, NG, T])
        qk_hi = sb("qk_hi", [P, 2, NG, T], F32R)
        qk_lo = sb("qk_lo", [P, 2, NG, T], F32R)
        q_stack = [sb(f"q_stack{i}", [P, NJ, NG, T], F32R) for i in range(2)]
        k_stack = [sb(f"k_stack{i}", [P, NJ, NG, T], F32R) for i in range(2)]
        v_sb = sb("v_sb", [P, 2, NC, H])
        neg_max = sb("neg_max", [P, NC, NH])
        neg_maxT = sb("neg_maxT", [P, T], F32R)
        probs_exp = [sb(f"probs_exp{i}", [P, NC, NH, T]) for i in range(1)]
        rsum = sb("rsum", [P, NG, T])
        oT = rsum
        x1 = sb("x1", [P, NC, H])
        stat2 = sb("stat2", [P, 2, 6])
        mv2 = sb("mv2", [P, 2, 2])
        nmean2 = sb("nmean2", [P, 2])
        rstd2 = sb("rstd2", [P, 2])
        xn2 = sb("xn2", [P, NC, H])
        xn2T = sb("xn2T", [P, NG, T])
        mod_b = sb("mod_b", [P, 2, H])
        resid = sb("resid", [P, B, NC, H])
        spare = iter(range(3, B))

        def in_resid(rows, a, width):
            return resid[0:rows, next(spare)].rearrange("p c h -> p (c h)")[:, 0:a * width]\
                .rearrange("p (a w) -> p a w", a=a)

        wqkv_nat = resid[:, 0:3].rearrange("p b c h -> p (b c) h")
        wo_nat = in_resid(P, NG, H)
        win_nat = in_resid(P, NG, H)
        bmat = in_resid(P, NG, S)
        a_twice = in_resid(S, 1, P)
        wprog_nat = in_resid(P, NG, PR)
        bo_row = in_resid(P, 1, H)
        bprog_row = in_resid(B, 1, H)
        yu = sb("yu", [P, T, B])
        prob_in = probs_exp[0][:, :, :, :].rearrange("p c h q -> p (c h q)")[:, 0:T // TQ * PR]
        yu_stage = xn
        out_tile = x_in

        unit = [stack.enter_context(nc.psum_tensor(f"unit{i}", [P, NJ, T], F32)) for i in range(2)]
        bank = [stack.enter_context(nc.psum_tensor(f"bank{i}", [P, 2, T], F32)) for i in range(4)]
        bank_x, bank_c, bank_o, bank_sum = bank

        mod_dram = nc.dram_tensor("mod_scratch", [B, H], F32).ap()

        weights_in = sem("weights_in")
        probs_in = sem("probs_in")
        mod_out = sem("mod_out")
        consts_pool = sem("consts_pool")
        consts_dve = sem("consts_dve")
        set_t = sem("set_t")
        set_e = sem("set_e")
        xc_in = sem2("xc_in")
        mod_in = sem2("mod_in")
        stats1_done = sem("stats1_done")
        norm1_done = sem("norm1_done")
        resid_pre = sem("resid_pre")
        xT_psum = sem("xT_psum")
        cT_psum = sem("cT_psum")
        xT_done = sem("xT_done")
        cT_done = sem("cT_done")
        q_psum = sem("q_psum")
        k_psum = sem("k_psum")
        v_psum = sem("v_psum")
        q_done = sem("q_done")
        k_done = sem("k_done")
        v_done = sem("v_done")
        q_split = sem("q_split")
        k_split = sem("k_split")
        stack_in = sem2("stack_in")
        score_psum = sem("score_psum")
        max_done = sem("max_done")
        maxT_psum = sem("maxT_psum")
        maxT_done = sem("maxT_done")
        logit_psum = sem("logit_psum")
        exp_done = sem("exp_done")
        pv_psum = sem("pv_psum")
        rsum_done = sem("rsum_done")
        oT_done = sem("oT_done")
        y_psum = sem("y_psum")
        x1_done = sem("x1_done")
        stats2_done = sem("stats2_done")
        norm2_done = sem("norm2_done")
        resid_done = sem("resid_done")
        x2T_psum = sem("x2T_psum")
        x2T_done = sem("x2T_done")
        u_psum = sem("u_psum")
        u_done = sem("u_done")
        dve_stat1 = sem("dve_stat1")
        dve_stat2 = sem("dve_stat2")
        dve_mv1 = sem("dve_mv1")
        dve_mv2 = sem("dve_mv2")
        pool_pow1 = sem("pool_pow1")
        pool_pow2 = sem("pool_pow2")
        z_ready = sem("z_ready")
        y_ready = sem("y_ready")
        stage_done = sem("stage_done")
        out_psum = sem("out_psum")
        out_done = sem("out_done")
        stored = sem2("stored")

        def wait(eng, s, value):
            if isinstance(value, int) and value <= 0:
                return
            eng.wait_ge(s, value)

        def wait_apart(eng, s, value):
            if isinstance(value, int) and value <= 0:
                return
            eng.wait_ge(s, value)
            if not isinstance(value, int):
                eng.nop(nofuse=True)

        def slots(eng, one_slot):
            for s in range(-4, 3):
                one_slot(s, s // 2, s % 2)
            with eng.Fori(1, B // 2 - 3) as i:
                one_slot(2 * i + 1, i, 1)
                one_slot(2 * i + 2, i + 1, 0)
            for s in range(B - 5, B + 1):
                one_slot(s, s // 2, s % 2)

        def has(s, lead):
            return not isinstance(s, int) or 0 <= s + lead < B

        block = stack.enter_context(nc.Block())

        @block.sync
        def _(sp):
            loads = [
                (wqkv_nat, W_qkv.rearrange("(r p) h -> p r h", p=P)),
                (wo_nat, W_o.rearrange("(r p) h -> p r h", p=P)),
                (win_nat, W_in.rearrange("(r p) h -> p r h", p=P)),
                (bmat, Bmat.rearrange("(r p) s -> p r s", p=P)),
                (a_twice[:, 0, 0:S], A), (a_twice[:, 0, S:P], A),
                (wprog_nat, W_prog.rearrange("(r p) s -> p r s", p=P)),
                (c2[0:S, :], Cmat), (c2[S:P, :], Cmat),
                (bo_row[:, 0], b_o.rearrange("(a h) -> a h", a=1).broadcast_to([P, H])),
                (bprog_row[:, 0], b_prog.rearrange("(a h) -> a h", a=1).broadcast_to([B, H])),
                (bv_nat[:], b_qkv[2 * H:3 * H].rearrange("(g p) -> p g", p=P)),
            ]
            for n, v in enumerate((g1, beta1, g2, beta2, b_in)):
                loads.append((vecs[:, n, :], v.rearrange("(g p) -> p g", p=P)))
            perm = b_qkv[0:2 * H].rearrange("(g j d) -> j d g", j=NJ, d=HD)
            for j in range(NJ):
                loads.append((bqk_perm[j:P:NJ, :], perm[j]))
            assert len(loads) == 21

            def load_xc(b, parity):
                wait_apart(sp, norm1_done, b - 1)
                wait_apart(sp, resid_pre, b - 1)
                sp.dma_start(x_in[:, parity], x[b].rearrange("(c p) h -> p c h", p=P)
                             if isinstance(b, int) else
                             x[bass.ds(b, 1)].rearrange("a (c p) h -> p (a c) h", p=P)).then_inc(xc_in[parity], 16)
                sp.dma_start(c_in[:, parity], ctx_in[b].rearrange("(c p) h -> p c h", p=P)
                             if isinstance(b, int) else
                             ctx_in[bass.ds(b, 1)].rearrange("a (c p) h -> p (a c) h", p=P)).then_inc(xc_in[parity], 16)

            sp.dma_start(prob_in, probs.rearrange("b (k t) s -> (b k) (t s)", k=TQ)).then_inc(probs_in, 16)
            for dst, src in loads:
                sp.dma_start(dst, src, allow_slow_non_contiguous=True).then_inc(weights_in, 16)
            def one_slot(s, pair, parity):
                other = 1 - parity
                if has(s, 4):
                    load_xc(s + 4, parity)
                if isinstance(s, int) and s == 0:
                    sp.wait_ge(set_e, 12)
                    sp.dma_start(mod_dram, mod_rows[:]).then_inc(mod_out, 16)
                    sp.wait_ge(mod_out, 16)
                if has(s, -1):
                    wait_apart(sp, resid_done, s - 2)
                    sp.dma_start(mod_b[:, other, :],
                                 (mod_dram[s - 1:s] if isinstance(s, int) else mod_dram[bass.ds(s - 1, 1)])
                                 .broadcast_to([P, H])).then_inc(mod_in[other], 16)
                if has(s, 1):
                    wait_apart(sp, logit_psum, 4 * s)
                    for n, (ready, dst) in enumerate(((q_split, q_stack), (k_split, k_stack))):
                        wait_apart(sp, ready, s + 2)
                        for r in range(4):
                            lo = (r % 2) if n == 0 else (r // 2)
                            src = (qk_lo if lo else qk_hi)[:, n].bitcast(F32).rearrange("p g t -> p (g t)")
                            sp.dma_start(dst[other][HD * r:HD * r + HD].bitcast(F32)
                                         .rearrange("p j g t -> p j (g t)"), src).then_inc(stack_in[other], 16)

            slots(sp, one_slot)

            with sp.Fori(0, B // 2) as i:
                for parity in range(2):
                    wait_apart(sp, out_done, 2 * i + parity + 1)
                    sp.dma_start(out[bass.ds(2 * i + parity, 1)].rearrange("a (c p) h -> p (a c) h", p=P),
                                 out_tile[:, parity]).then_inc(stored[parity], 16)
            for parity in range(2):
                sp.wait_ge(stored[parity], 16 * (B // 2))

        @block.gpsimd
        def _(pool):
            pool.memset(ident[:], 0.0).then_inc(consts_pool, 1)
            pool.memset(sel_batch[:], 1.0 / T).then_inc(consts_pool, 1)
            pool.wait_ge(consts_pool, 2)
            pool.affine_select(out=ident[:], in_=ident[:], compare_op=ALU.not_equal, fill=1.0, base=0,
                               pattern=[[-1, P]], channel_multiplier=1).then_inc(consts_pool, 1)
            pool.affine_select(out=sel_batch[:], in_=sel_batch[:], compare_op=ALU.is_ge, fill=0.0, base=0,
                               pattern=[[-TQ, B]], channel_multiplier=1).then_inc(consts_pool, 1)
            pool.wait_ge(consts_pool, 4)
            pool.affine_select(out=sel_batch[:], in_=sel_batch[:], compare_op=ALU.is_ge, fill=0.0, base=TQ - 1,
                               pattern=[[TQ, B]], channel_multiplier=-1).then_inc(consts_pool, 1)
            pool.memset(minus_half[:], -0.5).then_inc(consts_pool, 1)
            pool.wait_ge(consts_pool, 6)
            pool.wait_ge(set_e, 13)

            def one_slot(s, pair, parity):
                other = 1 - parity
                if has(s, 1):
                    if has(s, 0):
                        wait(pool, stack_in[parity], 128 * (pair + 1))
                    for n, (ready, split) in enumerate(((q_done, q_split), (k_done, k_split))):
                        wait(pool, ready, s + 2)
                        pool.tensor_tensor(qk_lo[:, n], qk32[:, n], qk_hi[:, n].bitcast(F32), ALU.subtract)\
                            .then_inc(split, 1)
                if has(s, 3):
                    wait(pool, stats1_done, s + 4)
                    pool.tensor_tensor(rstd1[:, other], rstd1[:, other], minus_half[:], ALU.pow)\
                        .then_inc(pool_pow1, 1)
                    wait(pool, pool_pow1, s + 4)
                    wait(pool, xT_psum, s + 2)
                    wait_apart(pool, cT_psum, s + 2)
                    for n, (src, dst) in enumerate(((x_in, xn), (c_in, cn))):
                        for c in range(NC):
                            m = 2 * n + c
                            last = pool.tensor_scalar(dst[:, other, c], src[:, other, c],
                                                      nmean1[:, other, m:m + 1], rstd1[:, other, m:m + 1],
                                                      ALU.add, ALU.mult)
                    last.then_inc(norm1_done, 1)
                    for c in range(NC):
                        dst = resid[:, s + 3, c] if isinstance(s, int) else resid[:, bass.ds(s + 3, 1), c]
                        a = x_in[:, other, c]
                        bb = bo[:]
                        if not isinstance(s, int):
                            a = a.unsqueeze(1)
                            bb = bb.unsqueeze(1)
                        last = pool.tensor_tensor(dst, a, bb, ALU.add)
                    last.then_inc(resid_pre, 1)
                if has(s, -1):
                    wait(pool, stats2_done, s)
                    pool.tensor_tensor(rstd2[:], rstd2[:], minus_half[:, 0:2], ALU.pow).then_inc(pool_pow2, 1)
                    wait(pool, pool_pow2, s)
                    wait_apart(pool, x2T_psum, s - 1)
                    for c in range(NC):
                        last = pool.tensor_scalar(xn2[:, c], x1[:, c], nmean2[:, c:c + 1], rstd2[:, c:c + 1],
                                                  ALU.add, ALU.mult)
                    last.then_inc(norm2_done, 1)
                if has(s, -1):
                    wait(pool, mod_in[other], 16 * (pair + parity))
                    for c in range(NC):
                        dst = resid[:, s - 1, c] if isinstance(s, int) else resid[:, bass.ds(s - 1, 1), c]
                        a, bb = x1[:, c], mod_b[:, other]
                        if not isinstance(s, int):
                            a, bb = a.unsqueeze(1), bb.unsqueeze(1)
                        last = pool.tensor_tensor(dst, a, bb, ALU.add)
                    last.then_inc(resid_done, 1)

            slots(pool, one_slot)

        @block.scalar
        def _(act):
            act.wait_ge(set_e, 13)

            def copy_v(s, pair, parity):
                if has(s, 1):
                    wait(act, v_psum, s + 2)
                    wait(act, pv_psum, s)
                    act.activation(v_sb[:, 1 - parity], bank_c[:], ACT.Identity).then_inc(v_done, 1)

            def one_slot(s, pair, parity):
                other = 1 - parity
                if has(s, 1):
                    wait(act, xT_psum, s + 2)
                    wait(act, q_psum, s + 1)
                    act.activation(xnT[:], bank_x[:], ACT.Identity).then_inc(xT_done, 1)
                    wait(act, cT_psum, s + 2)
                    wait(act, v_psum, s + 1)
                    act.activation(cnT[:], bank_c[:], ACT.Identity).then_inc(cT_done, 1)
                    for n, (ready, split, done, bnk) in enumerate(((q_psum, q_split, q_done, bank_x),
                                                                   (k_psum, k_split, k_done, bank_c))):
                        wait(act, ready, s + 2)
                        wait(act, split, s + 1)
                        if has(s, 0):
                            wait(act, stack_in[parity], 128 * (pair + 1))
                        for dst in (qk32, qk_hi):
                            for g in range(NG):
                                last = act.activation(dst[:, n, g], bnk[:, g], ACT.Identity,
                                                      bias=bqk[:, 2 * n + g:2 * n + g + 1])
                        last.then_inc(done, 1)
                if has(s, 0):
                    for n in range(4):
                        g, c = divmod(n, 2)
                        wait(act, logit_psum, 4 * s + n + 1)
                        if n == 0:
                            wait(act, pv_psum, s)
                        act.activation(probs_exp[0][:, c, NJ * g:NJ * g + NJ], unit[n % 2][:], ACT.Exp,
                                       scale=SCALE).then_inc(exp_done, 1)
                        if n == 0:
                            copy_v(s, pair, parity)
                else:
                    copy_v(s, pair, parity)
                if has(s, -1):
                    wait(act, x2T_psum, s)
                    wait(act, u_psum, s - 1)
                    act.activation(xn2T[:], bank_x[:], ACT.Identity).then_inc(x2T_done, 1)
                    wait(act, u_psum, s)
                    dst = yu[S:P, :, s - 1:s] if isinstance(s, int) else yu[S:P, :, bass.ds(s - 1, 1)]
                    act.activation(dst, bank_c[S:P, 0, :].unsqueeze(2), ACT.Identity,
                                   bias=bu[S:P, :]).then_inc(u_done, 1)

            slots(act, one_slot)

            with act.Fori(0, (T - 1) // SCAN_UNROLL) as i:
                for j in range(SCAN_UNROLL):
                    act.wait_ge(z_ready, SCAN_UNROLL * i + j + 1)
                    act.activation(yu[0:S, bass.ds(SCAN_UNROLL * i + j + 1, 1), :],
                                   bank[j % 3][0:S, 0:1, 0:B], ACT.Silu).then_inc(y_ready, 1)

        @block.vector
        def _(dve):
            dve.memset(ones_hd[:], 1.0).then_inc(consts_dve, 1)
            dve.memset(rsum[:], 0.0).then_inc(consts_dve, 1)
            dve.memset(yu[0:S, 0:1, :], 0.0).then_inc(y_ready, 1)
            dve.wait_ge(consts_dve, 2)
            dve.tensor_copy(neg_maxT[:], rsum[:, 0]).then_inc(consts_dve, 1)
            dve.wait_ge(consts_pool, 3)
            dve.tensor_copy(sel_head[:], ident[:, 0:NH]).then_inc(consts_dve, 1)
            dve.wait_ge(probs_in, 16)
            dve.tensor_reduce(prob_part[:], prob_in.rearrange("p (t s) -> p s t", s=PR), AX.X, ALU.add)\
                .then_inc(consts_dve, 1)
            dve.wait_ge(weights_in, 16 * 21)
            for r in range(6):
                dve.wait_ge(set_t, r // 2 + 1)
                src = (unit[0], unit[1], bank_x)[r // 2]
                flat = (src[:].rearrange("p a b -> p (a b)"))[:, 256 * (r % 2):256 * (r % 2) + 256]
                flat = flat.rearrange("p (k c) -> p k c", k=NG)
                dst = wT[:, :, P * r:P * r + P]
                if r < 4:
                    for k in range(NG):
                        ins = dve.tensor_copy(dst[:, k].rearrange("p (d j) -> p d j", j=NJ),
                                              flat[:, k].rearrange("p (j d) -> p d j", j=NJ))
                else:
                    ins = dve.tensor_copy(dst, flat)
                ins.then_inc(set_e, 1)
            dve.wait_ge(set_t, 4)
            for r in range(NG):
                ins = dve.tensor_copy(woT[:, :, P * r:P * r + P],
                                      bank_c[:, r].rearrange("p (k c) -> p k c", k=NG))
            ins.then_inc(set_e, 1)
            dve.wait_ge(set_t, 5)
            dve.tensor_copy(wprogT[:], bank_o[0:PR, 0, :])
            dve.tensor_copy(aT2[:], bank_o[:, 1, 0:S])
            dve.tensor_copy(wu_raw[:], bank_sum[:, 0, 0:NG * S].rearrange("p (k s) -> p k s", k=NG))
            dve.tensor_copy(prob_meanT[:], bank_sum[0:PR, 1, 0:B]).then_inc(set_e, 1)
            dve.wait_ge(set_t, 6)
            dve.tensor_tensor(bqk[:], bank_x[:, 0, 0:4], bqk_perm[:], ALU.add).then_inc(set_e, 1)
            dve.tensor_tensor(bv[:], bank_x[:, 0, 4:6], bv_nat[:], ALU.add).then_inc(set_e, 1)
            dve.tensor_copy(bu[S:P, :], bank_x[S:P, 0, 8:9]).then_inc(set_e, 1)
            dve.wait_ge(set_t, 7)
            dve.tensor_tensor(mod_rows[:], bank_o[0:B, 0, :], bprog_row[:, 0], ALU.add).then_inc(set_e, 1)
            dve.wait_ge(set_t, 8)
            dve.tensor_tensor(bo[:], bank_c[:, 0], bo_row[:, 0], ALU.add).then_inc(set_e, 1)
            for k in range(NG):
                dve.tensor_scalar(wT[:, k], wT[:, k], vecs[:, 0, k:k + 1], None, ALU.mult)
                ins = dve.tensor_scalar(wu[:, k], wu_raw[:, k], vecs[:, 2, k:k + 1], None, ALU.mult)
            ins.then_inc(set_e, 1)

            def one_slot(s, pair, parity):
                other = 1 - parity
                if has(s, 0):
                    for n in range(4):
                        g, c = divmod(n, 2)
                        wait(dve, score_psum, 4 * s + n + 1)
                        if n == 0:
                            wait(dve, maxT_psum, s)
                        dve.tensor_reduce(neg_max[:, c, NJ * g:NJ * g + NJ], unit[n % 2][:], AX.X, ALU.max,
                                          negate=True).then_inc(max_done, 1)
                    wait(dve, maxT_psum, s + 1)
                    wait(dve, logit_psum, 4 * s)
                    dve.tensor_copy(neg_maxT[0:NH, :], unit[1][0:NH, 0, :]).then_inc(maxT_done, 1)
                if has(s, -1):
                    wait(dve, pv_psum, s)
                    wait(dve, y_psum, s - 1)
                    dve.reciprocal(rsum[:], bank_sum[:]).then_inc(rsum_done, 1)
                    wait(dve, rsum_done, s)
                    dve.tensor_tensor(oT[:], bank_o[:], rsum[:], ALU.mult).then_inc(oT_done, 1)
                if has(s, 4):
                    wait(dve, xc_in[parity], 32 * (pair + 3))
                    wait(dve, stats1_done, s + 4)
                    wait(dve, norm1_done, s + 3)
                    for n, src in enumerate((x_in, c_in)):
                        for c in range(NC):
                            last = dve.bn_stats(stat1[:, 2 * n + c], src[:, parity, c])
                    last.then_inc(dve_stat1, 1)
                    wait_apart(dve, dve_stat1, s + 5)
                    for m in range(4):
                        last = dve.bn_aggr(mv1[:, parity, m], stat1[:, m])
                    last.then_inc(dve_mv1, 1)
                    wait(dve, dve_mv1, s + 5)
                    dve.tensor_scalar(nmean1[:, parity], mv1[:, parity, :, 0], -1.0, None, ALU.mult)
                    dve.tensor_scalar(rstd1[:, parity], mv1[:, parity, :, 1], EPS, None, ALU.add)\
                        .then_inc(stats1_done, 1)
                if has(s, -1):
                    wait(dve, y_psum, s)
                    wait(dve, resid_done, s - 1)
                    wait(dve, norm2_done, s - 1)
                    wait(dve, resid_pre, s)
                    if isinstance(s, int):
                        dve.tensor_tensor(x1[:], bank_x[:], resid[:, s - 1], ALU.add).then_inc(x1_done, 1)
                    else:
                        dve.tensor_tensor(x1[:].unsqueeze(1), bank_x[:].unsqueeze(1), resid[:, bass.ds(s - 1, 1)], ALU.add)\
                            .then_inc(x1_done, 1)
                    wait(dve, x1_done, s)
                    for c in range(NC):
                        last = dve.bn_stats(stat2[:, c], x1[:, c])
                    last.then_inc(dve_stat2, 1)
                    wait_apart(dve, dve_stat2, s)
                    for c in range(NC):
                        last = dve.bn_aggr(mv2[:, c], stat2[:, c])
                    last.then_inc(dve_mv2, 1)
                    wait(dve, norm2_done, s - 1)
                    wait_apart(dve, dve_mv2, s)
                    dve.tensor_scalar(nmean2[:], mv2[:, :, 0], -1.0, None, ALU.mult)
                    dve.tensor_scalar(rstd2[:], mv2[:, :, 1], EPS, None, ALU.add).then_inc(stats2_done, 1)

            slots(dve, one_slot)

            def stage(b, parity):
                for c in range(NC):
                    last = dve.tensor_copy(yu_stage[:, parity, c, 0:P], yu[:, P * c:P * c + P, bass.ds(b, 1)]
                                           .rearrange("p t a -> p (t a)"))
                last.then_inc(stage_done, 1)

            dve.wait_ge(resid_done, B)
            dve.wait_ge(y_ready, T)
            stage_first = [0, 1]
            for b in stage_first:
                for c in range(NC):
                    last = dve.tensor_copy(yu_stage[:, b, c, 0:P], yu[:, P * c:P * c + P, b])
                last.then_inc(stage_done, 1)

            def finish(i, parity, first, last_pair):
                b = 2 * i + parity
                dve.wait_ge(out_psum, b + 1)
                if not first:
                    dve.wait_ge(stored[parity], 16 * i)
                r = resid[:, b] if isinstance(b, int) else resid[:, bass.ds(b, 1)]
                o, ps = out_tile[:, parity], bank[parity][:]
                if not isinstance(b, int):
                    o, ps = o.unsqueeze(1), ps.unsqueeze(1)
                dve.tensor_tensor(o, ps, r, ALU.add).then_inc(out_done, 1)
                if not last_pair:
                    stage(b + 2, parity)

            for parity in range(2):
                finish(0, parity, True, False)
            with dve.Fori(1, B // 2 - 1) as i:
                for parity in range(2):
                    finish(i, parity, False, False)
            for parity in range(2):
                finish(B // 2 - 1, parity, False, True)

        @block.tensor
        def _(pe):
            pe.wait_ge(consts_pool, 3)
            pe.wait_ge(weights_in, 16 * 21)
            for r in range(6):
                dst = (unit[0], unit[1], bank_x)[r // 2][:].rearrange("p a b -> p (a b)")
                for k in range(NG):
                    c = 256 * (r % 2) + P * k
                    last = pe.transpose(dst[:, c:c + P], wqkv_nat[:, r, P * k:P * k + P], ident[:])
                if r % 2:
                    last.then_inc(set_t, 1)
            for r in range(NG):
                for k in range(NG):
                    last = pe.transpose(bank_c[:, r, P * k:P * k + P], wo_nat[:, r, P * k:P * k + P], ident[:])
            last.then_inc(set_t, 1)
            for r in range(NG):
                pe.transpose(bank_o[0:PR, 0, P * r:P * r + P], wprog_nat[:, r], ident[:])
            pe.transpose(bank_o[:, 1, 0:S], a_twice[:, 0], ident[0:S, 0:S])
            for k in range(NG):
                for m in range(NG):
                    pe.matmul(bank_sum[:, 0, S * k:S * k + S], win_nat[:, m, P * k:P * k + P], bmat[:, m],
                              start=(m == 0), stop=(m == NG - 1))
            pe.wait_ge(consts_dve, 5)
            pe.wait_ge(consts_pool, 5)
            pe.matmul(bank_sum[0:PR, 1, 0:B], prob_part[:], sel_batch[:], start=True, stop=True).then_inc(set_t, 1)
            pe.wait_ge(set_e, 8)
            for r in range(6):
                for k in range(NG):
                    pe.matmul(bank_x[:, 0, r:r + 1], wT[:, k, P * r:P * r + P], vecs[:, 1, k:k + 1],
                              start=(k == 0), stop=(k == NG - 1))
            for k in range(NG):
                pe.matmul(bank_x[S:P, 0, 8:9], wu_raw[:, k], vecs[:, 3, k:k + 1], start=(k == 0), stop=False)
            for m in range(NG):
                last = pe.matmul(bank_x[S:P, 0, 8:9], bmat[:, m], vecs[:, 4, m:m + 1], start=False, stop=(m == NG - 1))
            last.then_inc(set_t, 1)
            pe.matmul(bank_o[0:B, 0, :], prob_meanT[:], wprogT[:], start=True, stop=True).then_inc(set_t, 1)
            pe.wait_ge(set_e, 10)
            for k in range(NG):
                last = pe.matmul(bank_c[:, 0], bv[:, k:k + 1].broadcast_to([P, P]), woT[:, k],
                                 start=(k == 0), stop=(k == NG - 1))
            last.then_inc(set_t, 1)
            pe.wait_ge(set_e, 14)
            pe.wait_ge(consts_dve, 4)

            def transposes(src, other, dst):
                for c in range(NC):
                    for k in range(NG):
                        last = pe.transpose(dst[:, k, P * c:P * c + P], src[:, other, c, P * k:P * k + P], ident[:])
                return last

            def project(n, bnk, src):
                for g in range(NG):
                    for k in range(NG):
                        last = pe.matmul(bnk[:, g], wT[:, k, H * n + P * g:H * n + P * g + P], src[:, k],
                                         start=(k == 0), stop=(k == NG - 1))
                return last

            def one_slot(s, pair, parity):
                other = 1 - parity

                def scores(b, parity, n):
                    g, c = divmod(n, 2)
                    if n < 2:
                        wait(pe, exp_done, 4 * b - 1 + n)
                    else:
                        wait(pe, max_done, 4 * b + n - 1)
                    for j in range(NJ):
                        last = pe.matmul(unit[n % 2][:, j], q_stack[parity][:, j, g, P * c:P * c + P],
                                         k_stack[parity][:, j, g], start=True, stop=True)
                    last.then_inc(score_psum, 1)

                def logits(n):
                    g, c = divmod(n, 2)
                    if n == 1:
                        wait(pe, maxT_done, s + 1)
                    elif n > 1:
                        wait(pe, exp_done, 4 * s + n - 1)
                    for j in range(NJ):
                        pe.matmul(unit[n % 2][:, j], k_stack[parity][:, j, g, P * c:P * c + P],
                                  q_stack[parity][:, j, g], start=True, stop=False)
                        if n == 0 and j == 0:
                            wait(pe, maxT_done, s + 1)
                        last = pe.matmul(unit[n % 2][:, j], sel_head[:, NJ * g + j:NJ * g + j + 1].broadcast_to([P, P]),
                                         neg_maxT[:],
                                         start=False, stop=True)
                    last.then_inc(logit_psum, 1)

                def values(n):
                    g, c = divmod(n, 2)
                    wait(pe, exp_done, 4 * s + n + 1)
                    if n == 0:
                        wait(pe, v_done, s + 1)
                        wait(pe, oT_done, s)
                    for bnk in (bank_o, bank_sum):
                        for j in range(NJ):
                            h = NJ * g + j
                            w = v_sb[:, parity, c, HD * h:HD * h + HD] if bnk is bank_o else ones_hd[:]
                            last = pe.matmul(bnk[HD * j:HD * j + HD, g], w, probs_exp[0][:, c, h],
                                             start=(c == 0), stop=(c == NC - 1), tile_position=(0, HD * j))
                    if n == 3:
                        last.then_inc(pv_psum, 1)

                if has(s, 1):
                    wait(pe, norm1_done, s + 2)
                    wait(pe, q_done, s + 1)
                    wait(pe, x2T_done, s - 1)
                    transposes(xn, other, bank_x).then_inc(xT_psum, 1)
                    wait(pe, v_done, s + 1)
                    wait(pe, u_done, s - 1)
                    transposes(cn, other, bank_c).then_inc(cT_psum, 1)
                    wait(pe, xT_done, s + 2)
                    project(0, bank_x, xnT).then_inc(q_psum, 1)
                if has(s, 0):
                    scores(s, parity, 2)
                if has(s, 1):
                    wait(pe, cT_done, s + 2)
                    project(1, bank_c, cnT).then_inc(k_psum, 1)
                if has(s, 0):
                    scores(s, parity, 3)
                    wait(pe, max_done, 4 * s + 4)
                    for c in range(NC):
                        last = pe.transpose(unit[1][0:NH, 0, P * c:P * c + P], neg_max[:, c], ident[:])
                    last.then_inc(maxT_psum, 1)
                    logits(0)
                if has(s, 1):
                    wait(pe, k_done, s + 2)
                    for c in range(NC):
                        for k in range(NG):
                            last = pe.matmul(bank_c[:, c], cnT[:, k, P * c:P * c + P], wT[:, k, 2 * H:3 * H],
                                             start=(k == 0), stop=(k == NG - 1))
                    last.then_inc(v_psum, 1)
                if has(s, 0):
                    logits(1)
                if has(s, -1):
                    wait(pe, oT_done, s)
                    if has(s, 1):
                        wait(pe, q_done, s + 2)
                    else:
                        wait(pe, x2T_done, s - 1)
                    for c in range(NC):
                        for g in range(NG):
                            last = pe.matmul(bank_x[:, c], oT[:, g, P * c:P * c + P], woT[:, g],
                                             start=(g == 0), stop=(g == NG - 1))
                    last.then_inc(y_psum, 1)
                if has(s, 0):
                    values(0)
                    logits(2)
                    values(1)
                    logits(3)
                    values(2)
                    values(3)
                if has(s, -1):
                    wait(pe, norm2_done, s)
                    wait(pe, x1_done, s)
                    for c in range(NC):
                        for k in range(NG):
                            last = pe.transpose(bank_x[:, k, P * c:P * c + P], xn2[:, c, P * k:P * k + P], ident[:])
                    last.then_inc(x2T_psum, 1)
                if has(s, 1):
                    wait(pe, stack_in[other], 128 * (pair + parity + 1))
                    scores(s + 1, other, 0)
                    scores(s + 1, other, 1)
                if has(s, -1):
                    wait(pe, x2T_done, s)
                    if has(s, 1):
                        wait(pe, v_done, s + 2)
                    else:
                        wait(pe, u_done, s - 1)
                    for k in range(NG):
                        last = pe.matmul(bank_c[S:P, 0, :], wu[:, k], xn2T[:, k], start=(k == 0), stop=(k == NG - 1))
                    last.then_inc(u_psum, 1)

            slots(pe, one_slot)

            pe.wait_ge(u_done, B)
            with pe.Fori(0, (T - 1) // SCAN_UNROLL) as i:
                for j in range(SCAN_UNROLL):
                    pe.wait_ge(y_ready, SCAN_UNROLL * i + j + 1)
                    pe.matmul(bank[j % 3][0:S, 0:1, 0:B], aT2[:], yu[:, bass.ds(SCAN_UNROLL * i + j, 1), :],
                              start=True, stop=True).then_inc(z_ready, 1)

            def project_out(i, parity, first):
                b = 2 * i + parity
                pe.wait_ge(stage_done, b + 1)
                if not first:
                    pe.wait_ge(out_done, b - 1)
                for c in range(NC):
                    last = pe.matmul(bank[parity][:, c], yu_stage[:, parity, c, 0:P], c2[:], start=True, stop=True)
                last.then_inc(out_psum, 1)

            for parity in range(2):
                project_out(0, parity, True)
            with pe.Fori(1, B // 2) as i:
                for parity in range(2):
                    project_out(i, parity, False)


_INS = ["x", "ctx_1024", "itok_BxS2_4_31999", "ctxb_2048x64", "L0_xattn_A", "L0_xattn_Bmat", "L0_xattn_Cmat",
        "L0_xattn_W_in", "L0_xattn_b_in", "L0_xattn_W_qkv", "L0_xattn_b_qkv", "L0_xattn_W_o", "L0_xattn_b_o",
        "L0_xattn_W_prog", "L0_xattn_b_prog", "L0_xattn_g1", "L0_xattn_beta1", "L0_xattn_g2", "L0_xattn_beta2"]


def kernel(**inputs):
    import numpy as np
    import concourse.bacc as bacc
    from concourse import mybir as mb
    from concourse.bass_utils import run_bass_kernel_spmd

    nc = bacc.Bacc("TRN2", target_bir_lowering=False, num_devices=1)
    arrays, args = {}, []
    for name in _INS:
        a = np.ascontiguousarray(inputs[name])
        arrays[f"in_{name}"] = a
        args.append(nc.dram_tensor(f"in_{name}", a.shape, mb.dt.from_np(a.dtype), kind="ExternalInput").ap())
    out = nc.dram_tensor("out_0", inputs["x"].shape, mb.dt.float32, kind="ExternalOutput").ap()
    xattn_seq_kernel(nc, *args, out)
    result = run_bass_kernel_spmd(nc, [arrays], core_ids=[0])
    return result.results[0]["out_0"]
```

```python
from contextlib import ExitStack

import concourse.bass as bass
from concourse import mybir

F32 = mybir.dt.float32
F32R = mybir.dt.float32r
ALU = mybir.AluOpType
ACT = mybir.ActivationFunctionType
AX = mybir.AxisListType

P = 128
EPS = 1e-5


def xattn_seq_kernel(nc, x, ctx_in, itok, probs, A, Bmat, Cmat, W_in, b_in, W_qkv, b_qkv, W_o, b_o,
                     W_prog, b_prog, g1, beta1, g2, beta2, out):
    B, T, H = x.shape
    S = A.shape[0]
    PR = probs.shape[2]
    HD = 32
    NH = H // HD
    NG = H // P
    NJ = P // HD
    NC = T // P
    STACK = 7 * 16
    MR = 3 * HD
    SCALE = float(HD) ** -0.5
    TQ = P // B
    BS = 16
    TO = T // 4
    GB = 4
    NK = TO // BS
    assert 2 * S == P and NK * 2 * GB == B and NK % 2 == 0

    stack = ExitStack()
    with stack:
        def sb(name, shape, dt=F32):
            return stack.enter_context(nc.sbuf_tensor(name, shape, dt))

        def sem(name):
            return stack.enter_context(nc.semaphore(name))

        def sem2(name):
            return [sem(f"{name}{i}") for i in range(2)]

        ident = sb("ident", [P, P])
        zeros = sb("zeros", [NH, P])
        ones_hd = sb("ones_hd", [P, HD])
        minus_half = sb("minus_half", [P, 4])
        count_start = sb("count_start", [1, 5])
        wT = sb("wT", [P, NG, 3 * H])
        woT = sb("woT", [P, NG, H])
        wu_raw = sb("wu_raw", [P, NG, S])
        wu = sb("wu", [P, NG, S])
        aT2 = sb("aT2", [P, S])
        c2 = sb("c2", [P, H])
        wprogT = sb("wprogT", [PR, H])
        vecs = sb("vecs", [P, 5, NG])
        bqk_perm = sb("bqk_perm", [P, 4])
        bv_nat = sb("bv_nat", [P, NG])
        bqk = sb("bqk", [P, 4])
        bv = sb("bv", [P, NG])
        bu = sb("bu", [P, 1])
        bo = sb("bo", [P, H])
        sel_batch = sb("sel_batch", [P, B])
        prob_part = sb("prob_part", [P, PR])
        prob_meanT = sb("prob_meanT", [PR, B])
        mod_rows = sb("mod_rows", [B, H])

        x_in = sb("x_in", [P, 2, NC, H])
        c_in = sb("c_in", [P, 2, NC, H])
        stat1 = sb("stat1", [P, 4, 6])
        mv1 = sb("mv1", [P, 2, 4, 2])
        nmean1 = sb("nmean1", [P, 2, 4])
        rstd1 = sb("rstd1", [P, 2, 4])
        xn = sb("xn", [P, 2, NC, H])
        cn = sb("cn", [P, 2, NC, H])
        xnT = sb("xnT", [P, NG, T])
        cnT = sb("cnT", [P, NG, T])
        qk32 = sb("qk32", [P, 2, NG, T])
        qk_hi = sb("qk_hi", [P, 2, NG, T], F32R)
        qk_lo = sb("qk_lo", [P, 2, NG, T], F32R)
        q_stack = [sb(f"q_stack{i}", [P, NJ, NG, T], F32R) for i in range(2)]
        k_stack = [sb(f"k_stack{i}", [P, NJ, NG, T], F32R) for i in range(2)]
        v_sb = sb("v_sb", [P, 2, NC, H])
        neg_max = sb("neg_max", [P, NC, MR + NH])
        probs_exp = [sb(f"probs_exp{i}", [P, NC, NH, T]) for i in range(1)]
        rsum = sb("rsum", [P, NG, T])
        oT = rsum
        x1 = sb("x1", [P, NC, H])
        stat2 = sb("stat2", [P, 2, 6])
        mv2 = sb("mv2", [P, 2, 2])
        nmean2 = sb("nmean2", [P, 2])
        rstd2 = sb("rstd2", [P, 2])
        xn2 = sb("xn2", [P, NC, H])
        xn2T = sb("xn2T", [P, NG, T])
        mod_b = sb("mod_b", [P, 2, H])
        resid = sb("resid", [P, B, NC, H])
        spare = iter(range(3, B))

        def in_resid(rows, a, width):
            return resid[0:rows, next(spare)].rearrange("p c h -> p (c h)")[:, 0:a * width]\
                .rearrange("p (a w) -> p a w", a=a)

        wqkv_nat = resid[:, 0:3].rearrange("p b c h -> p (b c) h")
        wo_nat = in_resid(P, NG, H)
        win_nat = in_resid(P, NG, H)
        bmat = in_resid(P, NG, S)
        a_twice = in_resid(S, 1, P)
        wprog_nat = in_resid(P, NG, PR)
        bo_row = in_resid(P, 1, H)
        bprog_row = in_resid(B, 1, H)
        yu = sb("yu", [P, T, B])
        prob_in = probs_exp[0][:, :, :, :].rearrange("p c h q -> p (c h q)")[:, 0:T // TQ * PR]
        ring = cn[:].rearrange("p a c h -> p (a c h)").rearrange("p (t b) -> p t b", b=B)
        yu_stage = xn[:, 0].rearrange("p c h -> p (c h)").rearrange("p (b t) -> p b t", t=TO)
        out_tile = [x_in[:].rearrange("p a c h -> p (a c) h"), c_in[:].rearrange("p a c h -> p (a c) h")]

        unit = [stack.enter_context(nc.psum_tensor(f"unit{i}", [P, NJ, T], F32)) for i in range(2)]
        bank = [stack.enter_context(nc.psum_tensor(f"bank{i}", [P, 2, T], F32)) for i in range(4)]
        bank_x, bank_c = bank[0:2]
        bank_o = bank[2:4]

        mod_dram = nc.dram_tensor("mod_scratch", [B, H], F32).ap()

        weights_in = sem("weights_in")
        probs_in = sem("probs_in")
        mod_out = sem("mod_out")
        consts_pool = sem("consts_pool")
        consts_dve = sem("consts_dve")
        set_t = sem("set_t")
        set_e = sem("set_e")
        xc_in = sem2("xc_in")
        mod_in = sem2("mod_in")
        stats1_done = sem("stats1_done")
        norm1_done = sem("norm1_done")
        resid_pre = sem("resid_pre")
        xT_psum = sem("xT_psum")
        cT_psum = sem("cT_psum")
        xT_done = sem("xT_done")
        cT_done = sem("cT_done")
        q_psum = sem("q_psum")
        k_psum = sem("k_psum")
        v_psum = sem("v_psum")
        q_done = sem("q_done")
        k_done = sem("k_done")
        v_done = sem("v_done")
        q_split = sem("q_split")
        k_split = sem("k_split")
        stack_in = sem2("stack_in")
        score_psum = sem("score_psum")
        max_done = sem("max_done")
        maxT0_psum = sem("maxT0_psum")
        maxT1_psum = sem("maxT1_psum")
        maxT0_done = sem("maxT0_done")
        maxT1_done = sem("maxT1_done")
        logit_psum = sem("logit_psum")
        exp_done = sem("exp_done")
        pv_psum = sem("pv_psum")
        rsum_done = sem("rsum_done")
        oT_done = sem("oT_done")
        y_psum = sem("y_psum")
        x1_done = sem("x1_done")
        stats2_done = sem("stats2_done")
        norm2_done = sem("norm2_done")
        resid_done = sem("resid_done")
        x2T_psum = sem("x2T_psum")
        x2T_done = sem("x2T_done")
        u_psum = sem("u_psum")
        u_done = sem("u_done")
        dve_stat1 = sem("dve_stat1")
        dve_stat2 = sem("dve_stat2")
        dve_mv1 = sem("dve_mv1")
        dve_mv2 = sem("dve_mv2")
        pool_pow1 = sem("pool_pow1")
        pool_pow2 = sem("pool_pow2")
        z_ready = sem("z_ready")
        y_ready = sem("y_ready")
        u_loaded = sem("u_loaded")
        ring_free = sem("ring_free")
        stage_done = sem("stage_done")
        out_psum = sem("out_psum")
        out_done = sem2("out_done")
        stored = sem2("stored")

        def wait(eng, s, value):
            if isinstance(value, int) and value <= 0:
                return
            eng.wait_ge(s, value)

        def wait_apart(eng, s, value):
            if isinstance(value, int) and value <= 0:
                return
            eng.wait_ge(s, value)
            if not isinstance(value, int):
                eng.nop(nofuse=True)

        def slots(eng, one_slot):
            for s in range(-4, 3):
                one_slot(s, s // 2, s % 2)
            with eng.Fori(1, B // 2 - 3) as i:
                one_slot(2 * i + 1, i, 1)
                one_slot(2 * i + 2, i + 1, 0)
            for s in range(B - 5, B + 1):
                one_slot(s, s // 2, s % 2)

        def has(s, lead):
            return not isinstance(s, int) or 0 <= s + lead < B

        block = stack.enter_context(nc.Block())

        @block.sync
        def _(sp):
            loads = [
                (wqkv_nat, W_qkv.rearrange("(r p) h -> p r h", p=P)),
                (wo_nat, W_o.rearrange("(r p) h -> p r h", p=P)),
                (win_nat, W_in.rearrange("(r p) h -> p r h", p=P)),
                (bmat, Bmat.rearrange("(r p) s -> p r s", p=P)),
                (a_twice[:, 0, 0:S], A), (a_twice[:, 0, S:P], A),
                (wprog_nat, W_prog.rearrange("(r p) s -> p r s", p=P)),
                (c2[0:S, :], Cmat), (c2[S:P, :], Cmat),
                (bo_row[:, 0], b_o.rearrange("(a h) -> a h", a=1).broadcast_to([P, H])),
                (bprog_row[:, 0], b_prog.rearrange("(a h) -> a h", a=1).broadcast_to([B, H])),
                (bv_nat[:], b_qkv[2 * H:3 * H].rearrange("(g p) -> p g", p=P)),
            ]
            for n, v in enumerate((g1, beta1, g2, beta2, b_in)):
                loads.append((vecs[:, n, :], v.rearrange("(g p) -> p g", p=P)))
            perm = b_qkv[0:2 * H].rearrange("(g j d) -> j d g", j=NJ, d=HD)
            for j in range(NJ):
                loads.append((bqk_perm[j:P:NJ, :], perm[j]))
            assert len(loads) == 21

            def load_xc(b, parity):
                wait_apart(sp, norm1_done, b - 1)
                wait_apart(sp, resid_pre, b - 1)
                sp.dma_start(x_in[:, parity], x[b].rearrange("(c p) h -> p c h", p=P)
                             if isinstance(b, int) else
                             x[bass.ds(b, 1)].rearrange("a (c p) h -> p (a c) h", p=P)).then_inc(xc_in[parity], 16)
                sp.dma_start(c_in[:, parity], ctx_in[b].rearrange("(c p) h -> p c h", p=P)
                             if isinstance(b, int) else
                             ctx_in[bass.ds(b, 1)].rearrange("a (c p) h -> p (a c) h", p=P)).then_inc(xc_in[parity], 16)

            sp.dma_start(prob_in, probs.rearrange("b (k t) s -> (b k) (t s)", k=TQ)).then_inc(probs_in, 16)
            for dst, src in loads:
                sp.dma_start(dst, src, allow_slow_non_contiguous=True).then_inc(weights_in, 16)
            def one_slot(s, pair, parity):
                other = 1 - parity
                if has(s, 4):
                    load_xc(s + 4, parity)
                if isinstance(s, int) and s == 0:
                    sp.wait_ge(set_e, 12)
                    sp.dma_start(mod_dram, mod_rows[:]).then_inc(mod_out, 16)
                    sp.wait_ge(mod_out, 16)
                if has(s, -1):
                    wait_apart(sp, resid_done, s - 2)
                    sp.dma_start(mod_b[:, other, :],
                                 (mod_dram[s - 1:s] if isinstance(s, int) else mod_dram[bass.ds(s - 1, 1)])
                                 .broadcast_to([P, H])).then_inc(mod_in[other], 16)
                if has(s, 1):
                    wait_apart(sp, logit_psum, 4 * s)
                    sp.dma_start(q_stack[other][MR:MR + NH].bitcast(F32).rearrange("p j g (n w) -> p (j g n) w", w=P),
                                 zeros[:].unsqueeze(1).broadcast_to([NH, NJ * NG * T // P, P]))\
                        .then_inc(stack_in[other], 16)
                    for n, (ready, dst) in enumerate(((q_split, q_stack), (k_split, k_stack))):
                        wait_apart(sp, ready, s + 2)
                        for r in range(3):
                            lo = r == (1 if n == 0 else 2)
                            src = (qk_lo if lo else qk_hi)[:, n].bitcast(F32).rearrange("p g t -> p (g t)")
                            sp.dma_start(dst[other][HD * r:HD * r + HD].bitcast(F32)
                                         .rearrange("p j g t -> p j (g t)"), src).then_inc(stack_in[other], 16)

            slots(sp, one_slot)

            for c in range(T // TO):
                with sp.Fori(0, NK) as k:
                    for g in range(2):
                        wait_apart(sp, out_done[g], NK * c + k + 2)
                        sp.dma_start(out[bass.ds(2 * GB * k + GB * g, GB), TO * c:TO * c + TO].rearrange("b t h -> t b h"),
                                     out_tile[g][TO * (c % 2):TO * (c % 2) + TO]).then_inc(stored[g], 16)
            for g in range(2):
                sp.wait_ge(stored[g], 16 * (B // (2 * GB) * (T // TO) + 1))

        @block.gpsimd
        def _(pool):
            pool.memset(ident[:], 0.0).then_inc(consts_pool, 1)
            pool.memset(sel_batch[:], 1.0 / T).then_inc(consts_pool, 1)
            pool.wait_ge(consts_pool, 2)
            pool.affine_select(out=ident[:], in_=ident[:], compare_op=ALU.not_equal, fill=1.0, base=0,
                               pattern=[[-1, P]], channel_multiplier=1).then_inc(consts_pool, 1)
            pool.affine_select(out=sel_batch[:], in_=sel_batch[:], compare_op=ALU.is_ge, fill=0.0, base=0,
                               pattern=[[-TQ, B]], channel_multiplier=1).then_inc(consts_pool, 1)
            pool.wait_ge(consts_pool, 4)
            pool.affine_select(out=sel_batch[:], in_=sel_batch[:], compare_op=ALU.is_ge, fill=0.0, base=TQ - 1,
                               pattern=[[TQ, B]], channel_multiplier=-1).then_inc(consts_pool, 1)
            pool.wait_ge(consts_pool, 5)
            pool.memset(neg_max[:], 0.0).then_inc(consts_pool, 1)
            pool.memset(zeros[:], 0.0).then_inc(consts_pool, 1)
            pool.wait_ge(consts_pool, 7)
            for n in range(2):
                pool.tensor_copy(k_stack[n][MR:P], ident[MR:P, MR:MR + NH].rearrange("p (g j) -> p j g", j=NJ)
                                 .unsqueeze(3).broadcast_to([P - MR, NJ, NG, T])).then_inc(consts_pool, 1)
            pool.wait_ge(consts_pool, 9)
            pool.wait_ge(consts_dve, 2)
            pool.wait_ge(set_e, 13)

            def one_slot(s, pair, parity):
                other = 1 - parity
                if has(s, 1):
                    if has(s, 0):
                        wait(pool, stack_in[parity], STACK * (pair + 1))
                    for n, (ready, split) in enumerate(((q_done, q_split), (k_done, k_split))):
                        wait(pool, ready, s + 2)
                        pool.tensor_tensor(qk_lo[:, n], qk32[:, n], qk_hi[:, n].bitcast(F32), ALU.subtract)\
                            .then_inc(split, 1)
                if has(s, 3):
                    wait(pool, stats1_done, s + 4)
                    pool.tensor_tensor(rstd1[:, other], rstd1[:, other], minus_half[:], ALU.pow)\
                        .then_inc(pool_pow1, 1)
                    wait(pool, pool_pow1, s + 4)
                    wait(pool, xT_psum, s + 2)
                    wait_apart(pool, cT_psum, s + 2)
                    for n, (src, dst) in enumerate(((x_in, xn), (c_in, cn))):
                        for c in range(NC):
                            m = 2 * n + c
                            last = pool.tensor_scalar(dst[:, other, c], src[:, other, c],
                                                      nmean1[:, other, m:m + 1], rstd1[:, other, m:m + 1],
                                                      ALU.add, ALU.mult)
                    last.then_inc(norm1_done, 1)
                    for c in range(NC):
                        dst = resid[:, s + 3, c] if isinstance(s, int) else resid[:, bass.ds(s + 3, 1), c]
                        a = x_in[:, other, c]
                        bb = bo[:]
                        if not isinstance(s, int):
                            a = a.unsqueeze(1)
                            bb = bb.unsqueeze(1)
                        last = pool.tensor_tensor(dst, a, bb, ALU.add)
                    last.then_inc(resid_pre, 1)
                if has(s, -1):
                    wait(pool, stats2_done, s)
                    pool.tensor_tensor(rstd2[:], rstd2[:], minus_half[:, 0:2], ALU.pow).then_inc(pool_pow2, 1)
                    wait(pool, pool_pow2, s)
                    wait_apart(pool, x2T_psum, s - 1)
                    for c in range(NC):
                        last = pool.tensor_scalar(xn2[:, c], x1[:, c], nmean2[:, c:c + 1], rstd2[:, c:c + 1],
                                                  ALU.add, ALU.mult)
                    last.then_inc(norm2_done, 1)
                if has(s, -1):
                    wait(pool, mod_in[other], 16 * (pair + parity))
                    for c in range(NC):
                        dst = resid[:, s - 1, c] if isinstance(s, int) else resid[:, bass.ds(s - 1, 1), c]
                        a, bb = x1[:, c], mod_b[:, other]
                        if not isinstance(s, int):
                            a, bb = a.unsqueeze(1), bb.unsqueeze(1)
                        last = pool.tensor_tensor(dst, a, bb, ALU.add)
                    last.then_inc(resid_done, 1)

            slots(pool, one_slot)

            def load_u(k, h):
                wait_apart(pool, z_ready, BS * (k - 1) + 1)
                pool.tensor_copy(ring[S:P, BS * h:BS * h + BS, :], yu[S:P, bass.ds(BS * k, BS), :]).then_inc(u_loaded, 1)

            pool.wait_ge(resid_done, B)
            pool.wait_ge(cT_psum, B)
            pool.wait_ge(u_done, B)
            load_u(0, 0)
            load_u(1, 1)
            with pool.Fori(1, T // (2 * BS)) as i:
                for h in range(2):
                    load_u(2 * i + h, h)

        @block.scalar
        def _(act):
            act.wait_ge(set_e, 13)

            def split_in(s, pair, parity, n, ready, split, done):
                wait(act, ready, s + 2)
                wait(act, split, s + 1)
                if has(s, 0):
                    wait(act, stack_in[parity], STACK * (pair + 1))
                for dst in (qk32, qk_hi):
                    for g in range(NG):
                        last = act.activation(dst[:, n, g], bank_x[:, g], ACT.Identity,
                                              bias=bqk[:, 2 * n + g:2 * n + g + 1])
                last.then_inc(done, 1)

            def one_slot(s, pair, parity):
                other = 1 - parity
                if has(s, 1):
                    wait(act, xT_psum, s + 2)
                    wait(act, q_psum, s + 1)
                    act.activation(xnT[:], bank_x[:], ACT.Identity).then_inc(xT_done, 1)
                    wait(act, cT_psum, s + 2)
                    wait(act, k_psum, s + 1)
                    wait(act, v_psum, s + 1)
                    act.activation(cnT[:], bank_c[:], ACT.Identity).then_inc(cT_done, 1)
                    split_in(s, pair, parity, 0, q_psum, q_split, q_done)
                if has(s, 0):
                    wait(act, maxT0_psum, s + 1)
                    act.activation(q_stack[parity][MR:MR + NH, :, :, 0:P].rearrange("p j g t -> p (j g) t"),
                                   unit[0][MR:MR + NH, 0:1, 0:P].broadcast_to([NH, NH, P]), ACT.Identity)\
                        .then_inc(maxT0_done, 1)
                if has(s, 1):
                    wait(act, v_psum, s + 2)
                    wait(act, pv_psum, 2 * s)
                    act.activation(v_sb[:, 1 - parity], bank_c[:], ACT.Identity).then_inc(v_done, 1)
                if has(s, 1):
                    split_in(s, pair, parity, 1, k_psum, k_split, k_done)
                if has(s, 0):
                    for n in range(4):
                        g, c = divmod(n, 2)
                        wait(act, logit_psum, 4 * s + n + 1)
                        if n == 0:
                            wait(act, pv_psum, 2 * s)
                        act.activation(probs_exp[0][:, c, NJ * g:NJ * g + NJ], unit[n % 2][:], ACT.Exp,
                                       scale=SCALE).then_inc(exp_done, 1)
                if has(s, -1):
                    wait(act, x2T_psum, s)
                    wait(act, u_psum, s - 1)
                    act.activation(xn2T[:], bank_x[:], ACT.Identity).then_inc(x2T_done, 1)
                    wait(act, u_psum, s)
                    dst = yu[S:P, :, s - 1:s] if isinstance(s, int) else yu[S:P, :, bass.ds(s - 1, 1)]
                    act.activation(dst, bank_c[S:P, 0, :].unsqueeze(2), ACT.Identity,
                                   bias=bu[S:P, :]).then_inc(u_done, 1)

            slots(act, one_slot)

            act.wait_ge(x2T_done, B)
            act.wait_ge(u_psum, B)
            act.activation(xn2T[0:1, 0, 0:1], xn2T[0:1, 0, 0:1], ACT.Silu)
            with act.Fori(0, T // (2 * BS)) as i:
                for h in range(2):
                    act.wait_ge(ring_free, 2 * i + h + 1)
                    for j in range(BS):
                        act.wait_ge(z_ready, 2 * BS * i + BS * h + j + 1)
                        act.activation(ring[0:S, BS * h + j, :], bank[j % 2][0:S, 0, 0:B], ACT.Silu)\
                            .then_inc(y_ready, 1)

        @block.vector
        def _(dve):
            dve.memset(ones_hd[:], 1.0).then_inc(consts_dve, 1)
            dve.memset(minus_half[:], -0.5)
            dve.memset(rsum[:], 0.0).then_inc(consts_dve, 1)
            for g in range(2):
                dve.memset(count_start[:, 2 * g:2 * g + 1], 0.0).then_inc(out_done[g], 1)
                dve.memset(count_start[:, 2 * g + 1:2 * g + 2], 0.0).then_inc(stored[g], 16)
            dve.memset(count_start[:, 4:5], 0.0).then_inc(ring_free, 2)
            dve.wait_ge(consts_dve, 2)
            for n in range(2):
                dve.tensor_copy(q_stack[n][MR:P].rearrange("p j g t -> p j (g t)"),
                                rsum[MR:P].rearrange("p g t -> p (g t)").unsqueeze(1)
                                .broadcast_to([P - MR, NJ, NG * T])).then_inc(consts_dve, 1)
            dve.wait_ge(probs_in, 16)
            dve.tensor_reduce(prob_part[:], prob_in.rearrange("p (t s) -> p s t", s=PR), AX.X, ALU.add)\
                .then_inc(consts_dve, 1)
            dve.wait_ge(weights_in, 16 * 21)
            for r in range(6):
                dve.wait_ge(set_t, r // 2 + 1)
                src = (unit[0], unit[1], bank_x)[r // 2]
                flat = (src[:].rearrange("p a b -> p (a b)"))[:, 256 * (r % 2):256 * (r % 2) + 256]
                flat = flat.rearrange("p (k c) -> p k c", k=NG)
                dst = wT[:, :, P * r:P * r + P]
                if r < 4:
                    for k in range(NG):
                        ins = dve.tensor_copy(dst[:, k].rearrange("p (d j) -> p d j", j=NJ),
                                              flat[:, k].rearrange("p (j d) -> p d j", j=NJ))
                else:
                    ins = dve.tensor_copy(dst, flat)
                ins.then_inc(set_e, 1)
            dve.wait_ge(set_t, 4)
            for r in range(NG):
                ins = dve.tensor_copy(woT[:, :, P * r:P * r + P],
                                      bank_c[:, r].rearrange("p (k c) -> p k c", k=NG))
            ins.then_inc(set_e, 1)
            dve.wait_ge(set_t, 5)
            dve.tensor_copy(wprogT[:], bank[2][0:PR, 0, :])
            dve.tensor_copy(aT2[:], bank[2][:, 1, 0:S])
            dve.tensor_copy(wu_raw[:], bank[3][:, 0, 0:NG * S].rearrange("p (k s) -> p k s", k=NG))
            dve.tensor_copy(prob_meanT[:], bank[3][0:PR, 1, 0:B]).then_inc(set_e, 1)
            dve.wait_ge(set_t, 6)
            dve.tensor_tensor(bqk[:], bank_x[:, 0, 0:4], bqk_perm[:], ALU.add).then_inc(set_e, 1)
            dve.tensor_tensor(bv[:], bank_x[:, 0, 4:6], bv_nat[:], ALU.add).then_inc(set_e, 1)
            dve.tensor_copy(bu[S:P, :], bank_x[S:P, 0, 8:9]).then_inc(set_e, 1)
            dve.wait_ge(set_t, 7)
            dve.tensor_tensor(mod_rows[:], bank[2][0:B, 0, :], bprog_row[:, 0], ALU.add).then_inc(set_e, 1)
            dve.wait_ge(set_t, 8)
            dve.tensor_tensor(bo[:], bank_c[:, 0], bo_row[:, 0], ALU.add).then_inc(set_e, 1)
            for k in range(NG):
                dve.tensor_scalar(wT[:, k], wT[:, k], vecs[:, 0, k:k + 1], None, ALU.mult)
                ins = dve.tensor_scalar(wu[:, k], wu_raw[:, k], vecs[:, 2, k:k + 1], None, ALU.mult)
            ins.then_inc(set_e, 1)

            def one_slot(s, pair, parity):
                other = 1 - parity
                if has(s, 0):
                    for n in range(4):
                        g, c = divmod(n, 2)
                        wait(dve, score_psum, 4 * s + n + 1)
                        if n == 0:
                            wait(dve, maxT1_psum, s)
                        dve.tensor_reduce(neg_max[:, c, MR + NJ * g:MR + NJ * g + NJ], unit[n % 2][:], AX.X, ALU.max,
                                          negate=True).then_inc(max_done, 1)
                    wait(dve, maxT1_psum, s + 1)
                    dve.tensor_copy(q_stack[parity][MR:MR + NH, :, :, P:T].rearrange("p j g t -> p (j g) t"),
                                    unit[1][MR:MR + NH, 0:1, P:T].broadcast_to([NH, NH, P])).then_inc(maxT1_done, 1)
                if has(s, 4):
                    wait(dve, xc_in[parity], 32 * (pair + 3))
                    wait(dve, stats1_done, s + 4)
                    wait(dve, norm1_done, s + 3)
                    for n, src in enumerate((x_in, c_in)):
                        for c in range(NC):
                            last = dve.bn_stats(stat1[:, 2 * n + c], src[:, parity, c])
                    last.then_inc(dve_stat1, 1)
                    wait_apart(dve, dve_stat1, s + 5)
                    for m in range(4):
                        last = dve.bn_aggr(mv1[:, parity, m], stat1[:, m])
                    last.then_inc(dve_mv1, 1)
                    wait(dve, dve_mv1, s + 5)
                    dve.tensor_scalar(nmean1[:, parity], mv1[:, parity, :, 0], -1.0, None, ALU.mult)
                    dve.tensor_scalar(rstd1[:, parity], mv1[:, parity, :, 1], EPS, None, ALU.add)\
                        .then_inc(stats1_done, 1)
                if has(s, -1):
                    wait(dve, y_psum, s)
                    wait(dve, resid_done, s - 1)
                    wait(dve, norm2_done, s - 1)
                    wait(dve, resid_pre, s)
                    if isinstance(s, int):
                        dve.tensor_tensor(x1[:], bank_c[:], resid[:, s - 1], ALU.add).then_inc(x1_done, 1)
                    else:
                        dve.tensor_tensor(x1[:].unsqueeze(1), bank_c[:].unsqueeze(1), resid[:, bass.ds(s - 1, 1)], ALU.add)\
                            .then_inc(x1_done, 1)
                    wait(dve, x1_done, s)
                    for c in range(NC):
                        last = dve.bn_stats(stat2[:, c], x1[:, c])
                    last.then_inc(dve_stat2, 1)
                    wait_apart(dve, dve_stat2, s)
                    for c in range(NC):
                        last = dve.bn_aggr(mv2[:, c], stat2[:, c])
                    last.then_inc(dve_mv2, 1)
                    wait(dve, norm2_done, s - 1)
                    wait_apart(dve, dve_mv2, s)
                    dve.tensor_scalar(nmean2[:], mv2[:, :, 0], -1.0, None, ALU.mult)
                    dve.tensor_scalar(rstd2[:], mv2[:, :, 1], EPS, None, ALU.add).then_inc(stats2_done, 1)

                if has(s, 0):
                    for g in range(NG):
                        wait(dve, pv_psum, 2 * s + g + 1)
                        if g == 0:
                            wait(dve, y_psum, s)
                        dve.reciprocal(rsum[:, g], bank_o[g][:, 1]).then_inc(rsum_done, 1)
                        wait(dve, rsum_done, 2 * s + g + 1)
                        dve.tensor_tensor(oT[:, g], bank_o[g][:, 0], rsum[:, g], ALU.mult).then_inc(oT_done, 1)

            slots(dve, one_slot)

            def write_back(k, h):
                wait(dve, y_ready, BS * k + BS + 1)
                dve.tensor_copy(yu[0:S, bass.ds(BS * k, BS), :], ring[0:S, BS * h:BS * h + BS, :]).then_inc(ring_free, 1)

            def outputs(c, k):
                q = NK * c + k
                dve.wait_ge(ring_free, NK * (c + 1) + 2)
                dve.tensor_copy(yu_stage, yu[:, TO * c:TO * c + TO, bass.ds(2 * GB * k, 2 * GB)]
                                .rearrange("p t b -> p b t")).then_inc(stage_done, 1)
                rows = slice(TO * (c % 2), TO * (c % 2) + TO)
                for g in range(2):
                    wait_apart(dve, stored[g], 16 * q + 16)
                    wait_apart(dve, out_psum, 2 * q + g + 1)
                    dve.tensor_tensor(out_tile[g][rows], unit[g][rows],
                                      resid[rows, bass.ds(2 * GB * k + GB * g, GB), c // 2], ALU.add)\
                        .then_inc(out_done[g], 1)

            dve.wait_ge(resid_done, B)
            dve.wait_ge(cT_psum, B)
            dve.wait_ge(x2T_psum, B)
            dve.memset(ring[:, 2 * BS - 1, :], 0.0).then_inc(y_ready, 1)
            write_back(0, 0)
            write_back(1, 1)
            write_back(2, 0)
            write_back(3, 1)
            for c in range(T // TO - 1):
                with dve.Fori(0, NK // 2) as i:
                    for h in range(2):
                        outputs(c, 2 * i + h)
                        write_back(NK * (c + 1) + 2 * i + h, h)
            with dve.Fori(0, NK) as k:
                outputs(T // TO - 1, k)

        @block.tensor
        def _(pe):
            pe.wait_ge(consts_pool, 3)
            pe.wait_ge(weights_in, 16 * 21)
            for r in range(6):
                dst = (unit[0], unit[1], bank_x)[r // 2][:].rearrange("p a b -> p (a b)")
                for k in range(NG):
                    c = 256 * (r % 2) + P * k
                    last = pe.transpose(dst[:, c:c + P], wqkv_nat[:, r, P * k:P * k + P], ident[:])
                if r % 2:
                    last.then_inc(set_t, 1)
            for r in range(NG):
                for k in range(NG):
                    last = pe.transpose(bank_c[:, r, P * k:P * k + P], wo_nat[:, r, P * k:P * k + P], ident[:])
            last.then_inc(set_t, 1)
            for r in range(NG):
                pe.transpose(bank[2][0:PR, 0, P * r:P * r + P], wprog_nat[:, r], ident[:])
            pe.transpose(bank[2][:, 1, 0:S], a_twice[:, 0], ident[0:S, 0:S])
            for k in range(NG):
                for m in range(NG):
                    pe.matmul(bank[3][:, 0, S * k:S * k + S], win_nat[:, m, P * k:P * k + P], bmat[:, m],
                              start=(m == 0), stop=(m == NG - 1))
            pe.wait_ge(consts_dve, 5)
            pe.wait_ge(consts_pool, 5)
            pe.matmul(bank[3][0:PR, 1, 0:B], prob_part[:], sel_batch[:], start=True, stop=True).then_inc(set_t, 1)
            pe.wait_ge(set_e, 8)
            for r in range(6):
                for k in range(NG):
                    pe.matmul(bank_x[:, 0, r:r + 1], wT[:, k, P * r:P * r + P], vecs[:, 1, k:k + 1],
                              start=(k == 0), stop=(k == NG - 1))
            for k in range(NG):
                pe.matmul(bank_x[S:P, 0, 8:9], wu_raw[:, k], vecs[:, 3, k:k + 1], start=(k == 0), stop=False)
            for m in range(NG):
                last = pe.matmul(bank_x[S:P, 0, 8:9], bmat[:, m], vecs[:, 4, m:m + 1], start=False, stop=(m == NG - 1))
            last.then_inc(set_t, 1)
            pe.matmul(bank[2][0:B, 0, :], prob_meanT[:], wprogT[:], start=True, stop=True).then_inc(set_t, 1)
            pe.wait_ge(set_e, 10)
            for k in range(NG):
                last = pe.matmul(bank_c[:, 0], bv[:, k:k + 1].broadcast_to([P, P]), woT[:, k],
                                 start=(k == 0), stop=(k == NG - 1))
            last.then_inc(set_t, 1)
            pe.wait_ge(set_e, 14)
            pe.wait_ge(consts_dve, 4)

            def transposes(src, other, dst):
                for c in range(NC):
                    for k in range(NG):
                        last = pe.transpose(dst[:, k, P * c:P * c + P], src[:, other, c, P * k:P * k + P], ident[:])
                return last

            def project(n, bnk, src):
                for g in range(NG):
                    for k in range(NG):
                        last = pe.matmul(bnk[:, g], wT[:, k, H * n + P * g:H * n + P * g + P], src[:, k],
                                         start=(k == 0), stop=(k == NG - 1))
                return last

            def one_slot(s, pair, parity):
                other = 1 - parity

                def scores(b, parity, n):
                    g, c = divmod(n, 2)
                    if n < 2:
                        wait(pe, exp_done, 4 * b - 1 + n)
                    else:
                        wait(pe, max_done, 4 * b + n - 1)
                    for j in range(NJ):
                        last = pe.matmul(unit[n % 2][:, j], q_stack[parity][:, j, g, P * c:P * c + P],
                                         k_stack[parity][:, j, g], start=True, stop=True)
                    last.then_inc(score_psum, 1)

                def maxima(c, done):
                    wait(pe, max_done, 4 * s + 3 + c)
                    pe.transpose(unit[c][0:MR + NH, 0, P * c:P * c + P], neg_max[:, c], ident[:]).then_inc(done, 1)

                def logits(n):
                    g, c = divmod(n, 2)
                    if n == 0:
                        wait(pe, maxT0_done, s + 1)
                        wait(pe, maxT1_done, s + 1)
                    elif n > 1:
                        wait(pe, exp_done, 4 * s + n - 1)
                    for j in range(NJ):
                        last = pe.matmul(unit[n % 2][:, j], k_stack[parity][:, j, g, P * c:P * c + P],
                                         q_stack[parity][:, j, g], start=True, stop=True)
                    last.then_inc(logit_psum, 1)

                def values(n):
                    g, c = divmod(n, 2)
                    wait(pe, exp_done, 4 * s + n + 1)
                    if n == 0:
                        wait(pe, v_done, s + 1)
                        wait(pe, oT_done, 2 * s)
                    for m in range(2):
                        for j in range(NJ):
                            h = NJ * g + j
                            w = ones_hd[:] if m else v_sb[:, parity, c, HD * h:HD * h + HD]
                            last = pe.matmul(bank_o[g][HD * j:HD * j + HD, m], w, probs_exp[0][:, c, h],
                                             start=(c == 0 and m == 0), stop=(c == NC - 1 and m == 1),
                                             tile_position=(0, HD * j))
                    if c == 1:
                        last.then_inc(pv_psum, 1)

                if has(s, 1):
                    wait(pe, norm1_done, s + 2)
                    wait(pe, k_done, s + 1)
                    wait(pe, x2T_done, s - 1)
                    transposes(xn, other, bank_x).then_inc(xT_psum, 1)
                    wait(pe, v_done, s + 1)
                    wait(pe, u_done, s - 1)
                    transposes(cn, other, bank_c).then_inc(cT_psum, 1)
                if has(s, 0):
                    scores(s, parity, 2)
                if has(s, 1):
                    wait(pe, xT_done, s + 2)
                    project(0, bank_x, xnT).then_inc(q_psum, 1)
                if has(s, 0):
                    scores(s, parity, 3)
                    maxima(0, maxT0_psum)
                if has(s, 1):
                    wait(pe, cT_done, s + 2)
                    for c in range(NC):
                        for k in range(NG):
                            last = pe.matmul(bank_c[:, c], cnT[:, k, P * c:P * c + P], wT[:, k, 2 * H:3 * H],
                                             start=(k == 0), stop=(k == NG - 1))
                    last.then_inc(v_psum, 1)
                if has(s, 0):
                    maxima(1, maxT1_psum)
                if has(s, 1):
                    wait(pe, q_done, s + 2)
                    project(1, bank_x, cnT).then_inc(k_psum, 1)
                if has(s, 0):
                    logits(0)
                    logits(1)
                if has(s, -1):
                    wait(pe, oT_done, 2 * s)
                    if has(s, 1):
                        wait(pe, v_done, s + 2)
                    else:
                        wait(pe, u_done, s - 1)
                    for c in range(NC):
                        for g in range(NG):
                            last = pe.matmul(bank_c[:, c], oT[:, g, P * c:P * c + P], woT[:, g],
                                             start=(g == 0), stop=(g == NG - 1))
                    last.then_inc(y_psum, 1)
                if has(s, 0):
                    values(0)
                    logits(2)
                    values(1)
                    logits(3)
                    values(2)
                    values(3)
                if has(s, -1):
                    wait(pe, norm2_done, s)
                    if has(s, 1):
                        wait(pe, k_done, s + 2)
                    else:
                        wait(pe, x2T_done, s - 1)
                    for c in range(NC):
                        for k in range(NG):
                            last = pe.transpose(bank_x[:, k, P * c:P * c + P], xn2[:, c, P * k:P * k + P], ident[:])
                    last.then_inc(x2T_psum, 1)
                if has(s, 1):
                    wait(pe, stack_in[other], STACK * (pair + parity + 1))
                    scores(s + 1, other, 0)
                    scores(s + 1, other, 1)
                if has(s, -1):
                    wait(pe, x2T_done, s)
                    wait(pe, x1_done, s)
                    for k in range(NG):
                        last = pe.matmul(bank_c[S:P, 0, :], wu[:, k], xn2T[:, k], start=(k == 0), stop=(k == NG - 1))
                    last.then_inc(u_psum, 1)

            slots(pe, one_slot)

            def output(c, k, n):
                q, g = NK * c + k, n // GB
                if n == 0:
                    pe.wait_ge(stage_done, q + 1)
                if n % GB == 0:
                    pe.wait_ge(out_done[g], q + 1)
                prod = pe.matmul(unit[g][TO * (c % 2):TO * (c % 2) + TO, n % GB], yu_stage[:, n], c2[:],
                                 start=True, stop=True)
                if n % GB == GB - 1:
                    prod.then_inc(out_psum, 1)

            for c in range(T // TO):
                with pe.Fori(0, NK // 2) as i:
                    for h in range(2):
                        k = 2 * i + h
                        pe.wait_ge(u_loaded, NK * c + k + 1)
                        for j in range(BS):
                            pe.wait_ge(y_ready, TO * c + BS * k + j + 1)
                            pe.matmul(bank[j % 2][0:S, 0, 0:B], aT2[:], ring[:, (BS * h + j - 1) % (2 * BS), :],
                                      start=True, stop=True).then_inc(z_ready, 1)
                            if c > 0 and j >= BS - 2 * GB:
                                output(c - 1, k, j - (BS - 2 * GB))
            with pe.Fori(0, NK) as k:
                for n in range(2 * GB):
                    output(T // TO - 1, k, n)


_INS = ["x", "ctx_1024", "itok_BxS2_4_31999", "ctxb_2048x64", "L0_xattn_A", "L0_xattn_Bmat", "L0_xattn_Cmat",
        "L0_xattn_W_in", "L0_xattn_b_in", "L0_xattn_W_qkv", "L0_xattn_b_qkv", "L0_xattn_W_o", "L0_xattn_b_o",
        "L0_xattn_W_prog", "L0_xattn_b_prog", "L0_xattn_g1", "L0_xattn_beta1", "L0_xattn_g2", "L0_xattn_beta2"]


def kernel(**inputs):
    import numpy as np
    import concourse.bacc as bacc
    from concourse import mybir as mb
    from concourse.bass_utils import run_bass_kernel_spmd

    nc = bacc.Bacc("TRN2", target_bir_lowering=False, num_devices=1)
    arrays, args = {}, []
    for name in _INS:
        a = np.ascontiguousarray(inputs[name])
        arrays[f"in_{name}"] = a
        args.append(nc.dram_tensor(f"in_{name}", a.shape, mb.dt.from_np(a.dtype), kind="ExternalInput").ap())
    out = nc.dram_tensor("out_0", inputs["x"].shape, mb.dt.float32, kind="ExternalOutput").ap()
    xattn_seq_kernel(nc, *args, out)
    result = run_bass_kernel_spmd(nc, [arrays], core_ids=[0])
    return result.results[0]["out_0"]
```

```python
from contextlib import ExitStack

import concourse.bass as bass
from concourse import mybir

F32 = mybir.dt.float32
F32R = mybir.dt.float32r
ALU = mybir.AluOpType
ACT = mybir.ActivationFunctionType
AX = mybir.AxisListType

P = 128
EPS = 1e-5


def xattn_seq_kernel(nc, x, ctx_in, itok, probs, A, Bmat, Cmat, W_in, b_in, W_qkv, b_qkv, W_o, b_o,
                     W_prog, b_prog, g1, beta1, g2, beta2, out):
    B, T, H = x.shape
    S = A.shape[0]
    PR = probs.shape[2]
    HD = 32
    NH = H // HD
    NG = H // P
    NJ = P // HD
    NC = T // P
    STACK = 7 * 16
    MR = 3 * HD
    SCALE = float(HD) ** -0.5
    TQ = P // B
    BS = 16
    TO = T // 4
    GB = 4
    NK = TO // BS
    assert 2 * S == P and NK * 2 * GB == B and NK % 2 == 0

    stack = ExitStack()
    with stack:
        def sb(name, shape, dt=F32):
            return stack.enter_context(nc.sbuf_tensor(name, shape, dt))

        def sem(name):
            return stack.enter_context(nc.semaphore(name))

        def sem2(name):
            return [sem(f"{name}{i}") for i in range(2)]

        ident = sb("ident", [P, P])
        zeros = sb("zeros", [NH, P])
        ones_hd = sb("ones_hd", [P, HD])
        minus_half = sb("minus_half", [P, 4])
        count_start = sb("count_start", [1, 6])
        wT_hi = sb("wT_hi", [P, NG, 3 * H], F32R)
        wT_lo = sb("wT_lo", [P, NG, 3 * H], F32R)
        woT = sb("woT", [P, NG, H])
        wu = sb("wu", [P, NG, S])
        aT2 = sb("aT2", [P, S])
        c2 = sb("c2", [P, H])
        vecs = sb("vecs", [P, 5, NG])
        bqk_perm = sb("bqk_perm", [P, 4])
        bv_nat = sb("bv_nat", [P, NG])
        bqk = sb("bqk", [P, 4])
        bv = sb("bv", [P, NG])
        bu = sb("bu", [P, 1])
        bo = sb("bo", [P, H])
        sel_batch = sb("sel_batch", [P, B])
        prob_part = sb("prob_part", [P, PR])
        prob_meanT = sb("prob_meanT", [PR, B])
        mod_rows = sb("mod_rows", [B, H])

        x_in = sb("x_in", [P, 2, NC, H])
        c_in = sb("c_in", [P, 2, NC, H])
        stat1 = sb("stat1", [P, 4, 6])
        mv1 = sb("mv1", [P, 2, 4, 2])
        nmean1 = sb("nmean1", [P, 2, 4])
        rstd1 = sb("rstd1", [P, 2, 4])
        xn = sb("xn", [P, 2, NC, H])
        cn = sb("cn", [P, 2, NC, H])
        xnT_hi = sb("xnT_hi", [P, NG, T], F32R)
        xnT_lo = sb("xnT_lo", [P, NG, T], F32R)
        cnT_hi = sb("cnT_hi", [P, NG, T], F32R)
        cnT_lo = sb("cnT_lo", [P, NG, T], F32R)
        qk_hi = sb("qk_hi", [P, 2, NG, T], F32R)
        qk_lo = sb("qk_lo", [P, 2, NG, T], F32R)
        qk32 = sb("qk32", [P, 2, NG, T])
        q_stack = [sb(f"q_stack{i}", [P, NJ, NG, T], F32R) for i in range(2)]
        k_stack = [sb(f"k_stack{i}", [P, NJ, NG, T], F32R) for i in range(2)]
        v_sb = sb("v_sb", [P, 2, NC, H])
        neg_max = sb("neg_max", [P, NC, MR + NH])
        probs_exp = [sb(f"probs_exp{i}", [P, NJ, T]) for i in range(2)]
        rsum = sb("rsum", [P, NG, T])
        oT = rsum
        x1 = sb("x1", [P, NC, H])
        stat2 = sb("stat2", [P, 2, 6])
        mv2 = sb("mv2", [P, 2, 2])
        nmean2 = sb("nmean2", [P, 2])
        rstd2 = sb("rstd2", [P, 2])
        xn2 = sb("xn2", [P, NC, H])
        xn2T = sb("xn2T", [P, NG, T])
        mod_b = sb("mod_b", [P, 2, H])
        resid = sb("resid", [P, B, NC, H])
        spare = iter(range(3, B))

        def in_resid(rows, a, width):
            return resid[0:rows, next(spare)].rearrange("p c h -> p (c h)")[:, 0:a * width]\
                .rearrange("p (a w) -> p a w", a=a)

        wqkv_nat = resid[:, 0:3].rearrange("p b c h -> p (b c) h")
        wo_nat = in_resid(P, NG, H)
        win_nat = in_resid(P, NG, H)
        bmat = in_resid(P, NG, S)
        a_twice = in_resid(S, 1, P)
        wprog_nat = in_resid(P, NG, PR)
        bo_row = in_resid(P, 1, H)
        bprog_row = in_resid(B, 1, H)
        yu = sb("yu", [P, T, B])
        yu_free = yu[:].rearrange("p t b -> p (t b)")
        prob_in = yu_free[:, 0:T // TQ * PR]
        wT = yu_free[:, 4096:4096 + NG * 3 * H].rearrange("p (k c) -> p k c", k=NG)
        wu_raw = yu_free[:, 6144:6144 + NG * S].rearrange("p (k s) -> p k s", k=NG)
        wprogT = yu_free[0:PR, 7168:7168 + H]
        ring = cn[:].rearrange("p a c h -> p (a c h)").rearrange("p (t b) -> p t b", b=B)
        yu_stage = xn[:, 0].rearrange("p c h -> p (c h)").rearrange("p (b t) -> p b t", t=TO)
        out_tile = [x_in[:].rearrange("p a c h -> p (a c) h"), c_in[:].rearrange("p a c h -> p (a c) h")]

        unit = [stack.enter_context(nc.psum_tensor(f"unit{i}", [P, NJ, T], F32)) for i in range(2)]
        bank = [stack.enter_context(nc.psum_tensor(f"bank{i}", [P, 2, T], F32)) for i in range(4)]
        bank_x, bank_c = bank[0:2]
        bank_o = bank[2:4]

        mod_dram = nc.dram_tensor("mod_scratch", [B, H], F32).ap()

        weights_in = sem("weights_in")
        wqkv_in = sem("wqkv_in")
        vecs_in = sem("vecs_in")
        probs_in = sem("probs_in")
        w_ready = sem("w_ready")
        bias_psum = sem("bias_psum")
        bias_ready = sem("bias_ready")
        mod_out = sem("mod_out")
        consts_pool = sem("consts_pool")
        consts_dve = sem("consts_dve")
        set_t = sem("set_t")
        set_e = sem("set_e")
        xc_in = sem2("xc_in")
        mod_in = sem2("mod_in")
        stats1_done = sem("stats1_done")
        norm1_done = sem("norm1_done")
        resid_pre = sem("resid_pre")
        xT_psum = sem("xT_psum")
        cT_psum = sem("cT_psum")
        xT_done = sem("xT_done")
        cT_done = sem("cT_done")
        x_split = sem("x_split")
        c_split = sem("c_split")
        q_psum = sem("q_psum")
        k_psum = sem("k_psum")
        v_psum = sem("v_psum")
        q_done = sem("q_done")
        k_done = sem("k_done")
        v_done = sem("v_done")
        q_split = sem("q_split")
        k_split = sem("k_split")
        stack_in = sem2("stack_in")
        score_psum = sem("score_psum")
        max_done = sem("max_done")
        maxT0_psum = sem("maxT0_psum")
        maxT1_psum = sem("maxT1_psum")
        maxT0_done = sem("maxT0_done")
        maxT1_done = sem("maxT1_done")
        logit_psum = sem("logit_psum")
        exp_done = sem("exp_done")
        pv_psum = sem("pv_psum")
        rsum_done = sem("rsum_done")
        oT_done = sem("oT_done")
        y_psum = sem("y_psum")
        x1_done = sem("x1_done")
        stats2_done = sem("stats2_done")
        norm2_done = sem("norm2_done")
        resid_done = sem("resid_done")
        x2T_psum = sem("x2T_psum")
        x2T_done = sem("x2T_done")
        u_psum = sem("u_psum")
        u_done = sem("u_done")
        dve_stat1 = sem("dve_stat1")
        dve_stat2 = sem("dve_stat2")
        dve_mv1 = sem("dve_mv1")
        dve_mv2 = sem("dve_mv2")
        pool_pow1 = sem("pool_pow1")
        pool_pow2 = sem("pool_pow2")
        z_ready = sem("z_ready")
        y_ready = sem("y_ready")
        u_loaded = sem("u_loaded")
        ring_free = sem("ring_free")
        stage_done = sem("stage_done")
        out_psum = sem("out_psum")
        out_done = sem2("out_done")
        stored = sem2("stored")

        def wait(eng, s, value):
            if isinstance(value, int) and value <= 0:
                return
            eng.wait_ge(s, value)

        def wait_apart(eng, s, value):
            if isinstance(value, int) and value <= 0:
                return
            eng.wait_ge(s, value)
            if not isinstance(value, int):
                eng.nop(nofuse=True)

        def slots(eng, one_slot, first=-4):
            for s in range(first, 3):
                one_slot(s, s // 2, s % 2)
            with eng.Fori(1, B // 2 - 3) as i:
                one_slot(2 * i + 1, i, 1)
                one_slot(2 * i + 2, i + 1, 0)
            for s in range(B - 5, B + 2):
                one_slot(s, s // 2, s % 2)

        def has(s, lead):
            return not isinstance(s, int) or 0 <= s + lead < B

        block = stack.enter_context(nc.Block())

        @block.sync
        def _(sp):
            loads = [
                (wo_nat, W_o.rearrange("(r p) h -> p r h", p=P)),
                (win_nat, W_in.rearrange("(r p) h -> p r h", p=P)),
                (bmat, Bmat.rearrange("(r p) s -> p r s", p=P)),
                (a_twice[:, 0, 0:S], A), (a_twice[:, 0, S:P], A),
                (wprog_nat, W_prog.rearrange("(r p) s -> p r s", p=P)),
                (c2[0:S, :], Cmat), (c2[S:P, :], Cmat),
                (bo_row[:, 0], b_o.rearrange("(a h) -> a h", a=1).broadcast_to([P, H])),
                (bprog_row[:, 0], b_prog.rearrange("(a h) -> a h", a=1).broadcast_to([B, H])),
            ]
            early = [(bv_nat[:], b_qkv[2 * H:3 * H].rearrange("(g p) -> p g", p=P))]
            for n, v in enumerate((g1, beta1, g2, beta2, b_in)):
                early.append((vecs[:, n, :], v.rearrange("(g p) -> p g", p=P)))
            perm = b_qkv[0:2 * H].rearrange("(g j d) -> j d g", j=NJ, d=HD)
            for j in range(NJ):
                early.append((bqk_perm[j:P:NJ, :], perm[j]))
            assert len(early) == 10 and len(loads) == 10

            def load_xc(b, parity):
                wait_apart(sp, norm1_done, b - 1)
                wait_apart(sp, resid_pre, b - 1)
                sp.dma_start(x_in[:, parity], x[b].rearrange("(c p) h -> p c h", p=P)
                             if isinstance(b, int) else
                             x[bass.ds(b, 1)].rearrange("a (c p) h -> p (a c) h", p=P)).then_inc(xc_in[parity], 16)
                sp.dma_start(c_in[:, parity], ctx_in[b].rearrange("(c p) h -> p c h", p=P)
                             if isinstance(b, int) else
                             ctx_in[bass.ds(b, 1)].rearrange("a (c p) h -> p (a c) h", p=P)).then_inc(xc_in[parity], 16)

            sp.dma_start(wqkv_nat, W_qkv.rearrange("(r p) h -> p r h", p=P)).then_inc(wqkv_in, 16)
            load_xc(0, 0)
            for dst, src in early:
                sp.dma_start(dst, src, allow_slow_non_contiguous=True).then_inc(vecs_in, 16)
            load_xc(1, 1)
            sp.dma_start(prob_in, probs.rearrange("b (k t) s -> (b k) (t s)", k=TQ)).then_inc(probs_in, 16)
            for dst, src in loads:
                sp.dma_start(dst, src, allow_slow_non_contiguous=True).then_inc(weights_in, 16)
            def one_slot(s, pair, parity):
                other = 1 - parity
                filling = isinstance(s, int) and s < 0
                if has(s, 4) and not filling:
                    load_xc(s + 4, parity)
                if has(s, -1):
                    wait_apart(sp, resid_done, s - 2)
                    sp.dma_start(mod_b[:, other, :],
                                 (mod_dram[s - 1:s] if isinstance(s, int) else mod_dram[bass.ds(s - 1, 1)])
                                 .broadcast_to([P, H])).then_inc(mod_in[other], 16)
                if has(s, 1):
                    wait_apart(sp, logit_psum, 4 * s)
                    sp.dma_start(q_stack[other][MR:MR + NH].bitcast(F32).rearrange("p j g (n w) -> p (j g n) w", w=P),
                                 zeros[:].unsqueeze(1).broadcast_to([NH, NJ * NG * T // P, P]))\
                        .then_inc(stack_in[other], 16)
                    for n, (ready, dst) in enumerate(((q_split, q_stack), (k_split, k_stack))):
                        wait_apart(sp, ready, s + 2)
                        for r in range(3):
                            lo = r == (1 if n == 0 else 2)
                            src = (qk_lo if lo else qk_hi)[:, n].bitcast(F32).rearrange("p g t -> p (g t)")
                            sp.dma_start(dst[other][HD * r:HD * r + HD].bitcast(F32)
                                         .rearrange("p j g t -> p j (g t)"), src).then_inc(stack_in[other], 16)

                if isinstance(s, int) and s == -1:
                    load_xc(2, 0)
                    load_xc(3, 1)
                if isinstance(s, int) and s == 0:
                    sp.wait_ge(set_e, 10)
                    sp.dma_start(mod_dram, mod_rows[:]).then_inc(mod_out, 16)
                    sp.wait_ge(mod_out, 16)

            sp.wait_ge(consts_pool, 7)
            sp.wait_ge(consts_dve, 4)
            slots(sp, one_slot, first=-1)

            for c in range(T // TO):
                with sp.Fori(0, NK) as k:
                    for g in range(2):
                        wait_apart(sp, out_done[g], NK * c + k + 2)
                        sp.dma_start(out[bass.ds(2 * GB * k + GB * g, GB), TO * c:TO * c + TO].rearrange("b t h -> t b h"),
                                     out_tile[g][TO * (c % 2):TO * (c % 2) + TO]).then_inc(stored[g], 16)
            for g in range(2):
                sp.wait_ge(stored[g], 16 * (B // (2 * GB) * (T // TO) + 1))

        @block.gpsimd
        def _(pool):
            pool.memset(ident[:], 0.0).then_inc(consts_pool, 1)
            pool.memset(sel_batch[:], 1.0 / T).then_inc(consts_pool, 1)
            pool.wait_ge(consts_pool, 2)
            pool.affine_select(out=ident[:], in_=ident[:], compare_op=ALU.not_equal, fill=1.0, base=0,
                               pattern=[[-1, P]], channel_multiplier=1).then_inc(consts_pool, 1)
            pool.affine_select(out=sel_batch[:], in_=sel_batch[:], compare_op=ALU.is_ge, fill=0.0, base=0,
                               pattern=[[-TQ, B]], channel_multiplier=1).then_inc(consts_pool, 1)
            pool.wait_ge(consts_pool, 4)
            pool.affine_select(out=sel_batch[:], in_=sel_batch[:], compare_op=ALU.is_ge, fill=0.0, base=TQ - 1,
                               pattern=[[TQ, B]], channel_multiplier=-1).then_inc(consts_pool, 1)
            pool.wait_ge(consts_pool, 5)
            pool.memset(neg_max[:], 0.0).then_inc(consts_pool, 1)
            pool.memset(zeros[:], 0.0).then_inc(consts_pool, 1)
            pool.wait_ge(consts_pool, 7)
            for n in range(2):
                pool.tensor_copy(k_stack[n][MR:P], ident[MR:P, MR:MR + NH].rearrange("p (g j) -> p j g", j=NJ)
                                 .unsqueeze(3).broadcast_to([P - MR, NJ, NG, T])).then_inc(consts_pool, 1)
            pool.wait_ge(consts_pool, 9)
            pool.wait_ge(consts_dve, 2)

            def one_slot(s, pair, parity):
                other = 1 - parity

                def take_residual(b, buf):
                    wait(pool, stats1_done, b + 1)
                    for c in range(NC):
                        dst = resid[:, b, c] if isinstance(b, int) else resid[:, bass.ds(b, 1), c]
                        a = x_in[:, buf, c]
                        bb = bo[:]
                        if not isinstance(b, int):
                            a = a.unsqueeze(1)
                            bb = bb.unsqueeze(1)
                        last = pool.tensor_tensor(dst, a, bb, ALU.add)
                    last.then_inc(resid_pre, 1)

                if has(s, 1):
                    for n, (ready, split, hi, lo) in enumerate(((xT_done, x_split, xnT_hi, xnT_lo),
                                                                (cT_done, c_split, cnT_hi, cnT_lo))):
                        wait(pool, ready, s + 2)
                        pool.tensor_tensor(lo[:], qk32[:, n], hi[:].bitcast(F32), ALU.subtract)\
                            .then_inc(split, 1)
                    if has(s, 0):
                        wait(pool, stack_in[parity], STACK * (pair + 1))
                    for n, (ready, split) in enumerate(((q_done, q_split), (k_done, k_split))):
                        wait(pool, ready, s + 2)
                        pool.tensor_tensor(qk_lo[:, n], qk32[:, n], qk_hi[:, n].bitcast(F32), ALU.subtract)\
                            .then_inc(split, 1)
                if isinstance(s, int) and s == -1:
                    pool.wait_ge(set_e, 11)
                    take_residual(0, 0)
                    take_residual(1, 1)
                    take_residual(2, 0)
                elif has(s, 3) and has(s, 0):
                    take_residual(s + 3, other)
                if has(s, -1):
                    wait(pool, x1_done, s)
                    wait(pool, mod_in[other], 16 * (pair + parity))
                    for c in range(NC):
                        dst = resid[:, s - 1, c] if isinstance(s, int) else resid[:, bass.ds(s - 1, 1), c]
                        a, bb = x1[:, c], mod_b[:, other]
                        if not isinstance(s, int):
                            a, bb = a.unsqueeze(1), bb.unsqueeze(1)
                        last = pool.tensor_tensor(dst, a, bb, ALU.add)
                    last.then_inc(resid_done, 1)
                if has(s, -1):
                    wait(pool, stats2_done, s)
                    pool.tensor_tensor(rstd2[:], rstd2[:], minus_half[:, 0:2], ALU.pow).then_inc(pool_pow2, 1)
                    wait(pool, pool_pow2, s)
                    wait_apart(pool, x2T_psum, s - 1)
                    for c in range(NC):
                        last = pool.tensor_scalar(xn2[:, c], x1[:, c], nmean2[:, c:c + 1], rstd2[:, c:c + 1],
                                                  ALU.add, ALU.mult)
                    last.then_inc(norm2_done, 1)
                if has(s, 3):
                    wait(pool, stats1_done, s + 4)
                    pool.tensor_tensor(rstd1[:, other], rstd1[:, other], minus_half[:], ALU.pow)\
                        .then_inc(pool_pow1, 1)
                    wait(pool, pool_pow1, s + 4)
                    wait(pool, xT_psum, s + 2)
                    wait_apart(pool, cT_psum, s + 2)
                    for n, (src, dst) in enumerate(((x_in, xn), (c_in, cn))):
                        for c in range(NC):
                            m = 2 * n + c
                            last = pool.tensor_scalar(dst[:, other, c], src[:, other, c],
                                                      nmean1[:, other, m:m + 1], rstd1[:, other, m:m + 1],
                                                      ALU.add, ALU.mult)
                    last.then_inc(norm1_done, 1)

            slots(pool, one_slot)

            def load_u(k, h):
                wait_apart(pool, z_ready, BS * (k - 1) + 1)
                pool.tensor_copy(ring[S:P, BS * h:BS * h + BS, :], yu[S:P, bass.ds(BS * k, BS), :]).then_inc(u_loaded, 1)

            pool.wait_ge(resid_done, B)
            pool.wait_ge(cT_psum, B)
            pool.wait_ge(u_done, B)
            load_u(0, 0)
            load_u(1, 1)
            with pool.Fori(1, T // (2 * BS)) as i:
                for h in range(2):
                    load_u(2 * i + h, h)

        @block.scalar
        def _(act):
            act.wait_ge(consts_dve, 2)
            act.activation(count_start[:, 5:6], rsum[0:1, 0, 0:1], ACT.Identity)
            act.wait_ge(bias_ready, 2)

            def split_in(s, pair, parity, n, ready, used, done):
                wait(act, ready, s + 2)
                wait(act, used, s + 2)
                if has(s, 0):
                    wait(act, stack_in[parity], STACK * (pair + 1))
                for dst in (qk32, qk_hi):
                    for g in range(NG):
                        last = act.activation(dst[:, n, g], bank_x[:, g], ACT.Identity,
                                              bias=bqk[:, 2 * n + g:2 * n + g + 1])
                last.then_inc(done, 1)

            def one_slot(s, pair, parity):
                other = 1 - parity
                if has(s, 1):
                    wait(act, xT_psum, s + 2)
                    wait(act, q_psum, s + 1)
                    wait(act, q_split, s + 1)
                    act.activation(qk32[:, 0], bank_x[:], ACT.Identity)
                    act.activation(xnT_hi[:], bank_x[:], ACT.Identity).then_inc(xT_done, 1)
                if has(s, -2):
                    wait(act, u_psum, s - 1)
                    dst = yu[S:P, :, s - 2:s - 1] if isinstance(s, int) else yu[S:P, :, bass.ds(s - 2, 1)]
                    act.activation(dst, bank_o[0][S:P, 0, :].unsqueeze(2), ACT.Identity,
                                   bias=bu[S:P, :]).then_inc(u_done, 1)
                if has(s, 1):
                    wait(act, cT_psum, s + 2)
                    wait(act, k_psum, s + 1)
                    wait(act, v_psum, s + 1)
                    wait(act, k_split, s + 1)
                    act.activation(qk32[:, 1], bank_c[:], ACT.Identity)
                    act.activation(cnT_hi[:], bank_c[:], ACT.Identity).then_inc(cT_done, 1)
                    split_in(s, pair, parity, 0, q_psum, x_split, q_done)
                if has(s, 0):
                    wait(act, maxT0_psum, s + 1)
                    act.activation(q_stack[parity][MR:MR + NH, :, :, 0:P].rearrange("p j g t -> p (j g) t"),
                                   unit[0][MR:MR + NH, 0:1, 0:P].broadcast_to([NH, NH, P]), ACT.Identity)\
                        .then_inc(maxT0_done, 1)
                if has(s, 1):
                    wait(act, v_psum, s + 2)
                    wait(act, pv_psum, 4 * s)
                    act.activation(v_sb[:, 1 - parity], bank_c[:], ACT.Identity).then_inc(v_done, 1)
                if has(s, 1):
                    split_in(s, pair, parity, 1, k_psum, c_split, k_done)
                if has(s, 0):
                    for n in range(4):
                        g, c = divmod(n, 2)
                        wait(act, logit_psum, 4 * s + n + 1)
                        wait(act, pv_psum, 4 * s + n - 1)
                        act.activation(probs_exp[n % 2][:], unit[n % 2][:], ACT.Exp,
                                       scale=SCALE).then_inc(exp_done, 1)
                if has(s, -1):
                    wait(act, x2T_psum, s)
                    wait(act, u_psum, s - 1)
                    act.activation(xn2T[:], bank_x[:], ACT.Identity).then_inc(x2T_done, 1)

            slots(act, one_slot)

            act.wait_ge(x2T_done, B)
            act.wait_ge(u_psum, B)
            act.activation(xn2T[0:1, 0, 0:1], xn2T[0:1, 0, 0:1], ACT.Silu)
            with act.Fori(0, T // (2 * BS)) as i:
                for h in range(2):
                    act.wait_ge(ring_free, 2 * i + h + 1)
                    for j in range(BS):
                        act.wait_ge(z_ready, 2 * BS * i + BS * h + j + 1)
                        act.activation(ring[0:S, BS * h + j, :], bank[j % 2][0:S, 0, 0:B], ACT.Silu)\
                            .then_inc(y_ready, 1)

        @block.vector
        def _(dve):
            dve.memset(ones_hd[:], 1.0).then_inc(consts_dve, 1)
            dve.memset(minus_half[:], -0.5)
            dve.memset(rsum[:], 0.0).then_inc(consts_dve, 1)
            for g in range(2):
                dve.memset(count_start[:, 2 * g:2 * g + 1], 0.0).then_inc(out_done[g], 1)
                dve.memset(count_start[:, 2 * g + 1:2 * g + 2], 0.0).then_inc(stored[g], 16)
            dve.memset(count_start[:, 4:5], 0.0).then_inc(ring_free, 2)
            dve.wait_ge(consts_dve, 2)
            for n in range(2):
                dve.tensor_copy(q_stack[n][MR:P].rearrange("p j g t -> p j (g t)"),
                                rsum[MR:P].rearrange("p g t -> p (g t)").unsqueeze(1)
                                .broadcast_to([P - MR, NJ, NG * T])).then_inc(consts_dve, 1)
            def statistics(b, pair, parity):
                wait(dve, xc_in[parity], 32 * (pair + 1))
                wait(dve, stats1_done, b)
                wait(dve, norm1_done, b - 1)
                for n, src in enumerate((x_in, c_in)):
                    for c in range(NC):
                        last = dve.bn_stats(stat1[:, 2 * n + c], src[:, parity, c])
                last.then_inc(dve_stat1, 1)
                wait_apart(dve, dve_stat1, b + 1)
                for m in range(4):
                    last = dve.bn_aggr(mv1[:, parity, m], stat1[:, m])
                last.then_inc(dve_mv1, 1)
                wait(dve, dve_mv1, b + 1)
                dve.tensor_scalar(nmean1[:, parity], mv1[:, parity, :, 0], -1.0, None, ALU.mult)
                dve.tensor_scalar(rstd1[:, parity], mv1[:, parity, :, 1], EPS, None, ALU.add)\
                    .then_inc(stats1_done, 1)

            statistics(0, 0, 0)
            for r in range(6):
                dve.wait_ge(set_t, r // 2 + 1)
                src = (unit[0], unit[1], bank_x)[r // 2]
                flat = (src[:].rearrange("p a b -> p (a b)"))[:, 256 * (r % 2):256 * (r % 2) + 256]
                flat = flat.rearrange("p (k c) -> p k c", k=NG)
                dst = wT[:, :, P * r:P * r + P]
                if r < 4:
                    for k in range(NG):
                        ins = dve.tensor_copy(dst[:, k].rearrange("p (d j) -> p d j", j=NJ),
                                              flat[:, k].rearrange("p (j d) -> p d j", j=NJ))
                else:
                    ins = dve.tensor_copy(dst, flat)
                ins.then_inc(set_e, 1)
            dve.wait_ge(vecs_in, 16 * 10)
            dve.wait_ge(set_e, 6)
            for k in range(NG):
                dve.tensor_scalar(wT_hi[:, k], wT[:, k], vecs[:, 0, k:k + 1], None, ALU.mult).then_inc(w_ready, 1)
            dve.wait_ge(w_ready, NG)
            for k in range(NG):
                dve.scalar_tensor_tensor(wT_lo[:, k], wT[:, k], vecs[:, 0, k:k + 1], wT_hi[:, k].bitcast(F32),
                                         ALU.mult, ALU.subtract).then_inc(w_ready, 1)
            dve.wait_ge(bias_psum, 1)
            dve.tensor_tensor(bqk[:], bank[3][:, 0, 0:4], bqk_perm[:], ALU.add).then_inc(bias_ready, 1)
            dve.tensor_tensor(bv[:], bank[3][:, 0, 4:6], bv_nat[:], ALU.add).then_inc(bias_ready, 1)
            statistics(1, 0, 1)
            dve.wait_ge(probs_in, 16)
            dve.tensor_reduce(prob_part[:], prob_in.rearrange("p (t s) -> p s t", s=PR), AX.X, ALU.add)\
                .then_inc(consts_dve, 1)
            dve.wait_ge(weights_in, 16 * 10)
            dve.wait_ge(set_t, 4)
            for r in range(NG):
                ins = dve.tensor_copy(woT[:, :, P * r:P * r + P],
                                      unit[0][:, r].rearrange("p (k c) -> p k c", k=NG))
            ins.then_inc(set_e, 1)
            dve.wait_ge(set_t, 5)
            dve.tensor_copy(wprogT, bank[2][0:PR, 0, :])
            dve.tensor_copy(aT2[:], bank[2][:, 1, 0:S])
            dve.tensor_copy(wu_raw, bank[3][:, 0, 0:NG * S].rearrange("p (k s) -> p k s", k=NG))
            dve.tensor_copy(prob_meanT[:], bank[3][0:PR, 1, 0:B]).then_inc(set_e, 1)
            dve.wait_ge(set_t, 6)
            dve.tensor_copy(bu[S:P, :], unit[1][S:P, 0, 0:1]).then_inc(set_e, 1)
            dve.wait_ge(set_t, 7)
            dve.tensor_tensor(mod_rows[:], bank[2][0:B, 0, :], bprog_row[:, 0], ALU.add).then_inc(set_e, 1)
            dve.wait_ge(set_t, 8)
            dve.tensor_tensor(bo[:], unit[1][:, 2], bo_row[:, 0], ALU.add).then_inc(set_e, 1)
            for k in range(NG):
                ins = dve.tensor_scalar(wu[:, k], wu_raw[:, k], vecs[:, 2, k:k + 1], None, ALU.mult)
            ins.then_inc(set_e, 1)

            def one_slot(s, pair, parity):
                other = 1 - parity
                def invert(b, g):
                    wait(dve, pv_psum, 4 * b + 2 * g + 2)
                    if g == 0:
                        wait(dve, y_psum, b)
                    dve.reciprocal(rsum[:, g], bank_o[g][:, 1]).then_inc(rsum_done, 1)

                def normalise(b, g):
                    wait(dve, rsum_done, 2 * b + g + 1)
                    dve.tensor_tensor(oT[:, g], bank_o[g][:, 0], rsum[:, g], ALU.mult).then_inc(oT_done, 1)

                if has(s, -1) and not has(s, 0):
                    normalise(s - 1, 1)
                if has(s, 0):
                    for n in range(4):
                        g, c = divmod(n, 2)
                        if n == 3 and has(s, -1):
                            normalise(s - 1, 1)
                        wait(dve, score_psum, 4 * s + n + 1)
                        if n == 0:
                            wait(dve, maxT1_psum, s)
                        dve.tensor_reduce(neg_max[:, c, MR + NJ * g:MR + NJ * g + NJ], unit[n % 2][:], AX.X, ALU.max,
                                          negate=True).then_inc(max_done, 1)
                    wait(dve, maxT1_psum, s + 1)
                    dve.tensor_copy(q_stack[parity][MR:MR + NH, :, :, P:T].rearrange("p j g t -> p (j g) t"),
                                    unit[1][MR:MR + NH, 0:1, P:T].broadcast_to([NH, NH, P])).then_inc(maxT1_done, 1)
                if has(s, 4):
                    statistics(s + 4, pair + 2, parity)
                if has(s, -1):
                    wait(dve, y_psum, s)
                    wait(dve, resid_done, s - 1)
                    wait(dve, norm2_done, s - 1)
                    wait(dve, resid_pre, s)
                    if isinstance(s, int):
                        dve.tensor_tensor(x1[:], bank_c[:], resid[:, s - 1], ALU.add).then_inc(x1_done, 1)
                    else:
                        dve.tensor_tensor(x1[:].unsqueeze(1), bank_c[:].unsqueeze(1), resid[:, bass.ds(s - 1, 1)], ALU.add)\
                            .then_inc(x1_done, 1)
                    wait(dve, x1_done, s)
                    for c in range(NC):
                        last = dve.bn_stats(stat2[:, c], x1[:, c])
                    last.then_inc(dve_stat2, 1)
                    wait_apart(dve, dve_stat2, s)
                    for c in range(NC):
                        last = dve.bn_aggr(mv2[:, c], stat2[:, c])
                    last.then_inc(dve_mv2, 1)
                    wait(dve, norm2_done, s - 1)
                    wait_apart(dve, dve_mv2, s)
                    dve.tensor_scalar(nmean2[:], mv2[:, :, 0], -1.0, None, ALU.mult)
                    dve.tensor_scalar(rstd2[:], mv2[:, :, 1], EPS, None, ALU.add).then_inc(stats2_done, 1)

                if has(s, 0):
                    invert(s, 0)
                    normalise(s, 0)
                    invert(s, 1)

            slots(dve, one_slot, first=-2)

            def write_back(k, h):
                wait(dve, y_ready, BS * k + BS + 1)
                dve.tensor_copy(yu[0:S, bass.ds(BS * k, BS), :], ring[0:S, BS * h:BS * h + BS, :]).then_inc(ring_free, 1)

            def outputs(c, k):
                q = NK * c + k
                dve.wait_ge(ring_free, NK * (c + 1) + 2)
                dve.tensor_copy(yu_stage, yu[:, TO * c:TO * c + TO, bass.ds(2 * GB * k, 2 * GB)]
                                .rearrange("p t b -> p b t")).then_inc(stage_done, 1)
                rows = slice(TO * (c % 2), TO * (c % 2) + TO)
                for g in range(2):
                    wait_apart(dve, stored[g], 16 * q + 16)
                    wait_apart(dve, out_psum, 2 * q + g + 1)
                    dve.tensor_tensor(out_tile[g][rows], unit[g][rows],
                                      resid[rows, bass.ds(2 * GB * k + GB * g, GB), c // 2], ALU.add)\
                        .then_inc(out_done[g], 1)

            dve.wait_ge(resid_done, B)
            dve.wait_ge(cT_psum, B)
            dve.wait_ge(x2T_psum, B)
            dve.memset(ring[:, 2 * BS - 1, :], 0.0).then_inc(y_ready, 1)
            write_back(0, 0)
            write_back(1, 1)
            write_back(2, 0)
            write_back(3, 1)
            for c in range(T // TO - 1):
                with dve.Fori(0, NK // 2) as i:
                    for h in range(2):
                        outputs(c, 2 * i + h)
                        write_back(NK * (c + 1) + 2 * i + h, h)
            with dve.Fori(0, NK) as k:
                outputs(T // TO - 1, k)

        @block.tensor
        def _(pe):
            pe.wait_ge(consts_pool, 3)
            pe.wait_ge(wqkv_in, 16)
            for r in range(6):
                dst = (unit[0], unit[1], bank_x)[r // 2][:].rearrange("p a b -> p (a b)")
                for k in range(NG):
                    c = 256 * (r % 2) + P * k
                    last = pe.transpose(dst[:, c:c + P], wqkv_nat[:, r, P * k:P * k + P], ident[:])
                if r % 2:
                    last.then_inc(set_t, 1)
            pe.wait_ge(set_e, 6)
            pe.wait_ge(vecs_in, 16 * 10)
            for r in range(6):
                for k in range(NG):
                    last = pe.matmul(bank[3][:, 0, r:r + 1], wT[:, k, P * r:P * r + P], vecs[:, 1, k:k + 1],
                                     start=(k == 0), stop=(k == NG - 1))
            last.then_inc(bias_psum, 1)
            pe.wait_ge(w_ready, 2 * NG)
            pe.wait_ge(consts_dve, 4)

            def setup_rest():
                pe.wait_ge(weights_in, 16 * 10)
                for r in range(NG):
                    for k in range(NG):
                        last = pe.transpose(unit[0][:, r, P * k:P * k + P], wo_nat[:, r, P * k:P * k + P], ident[:])
                last.then_inc(set_t, 1)
                for r in range(NG):
                    pe.transpose(bank[2][0:PR, 0, P * r:P * r + P], wprog_nat[:, r], ident[:])
                pe.transpose(bank[2][:, 1, 0:S], a_twice[:, 0], ident[0:S, 0:S])
                pe.wait_ge(bias_ready, 2)
                for k in range(NG):
                    for m in range(NG):
                        pe.matmul(bank[3][:, 0, S * k:S * k + S], win_nat[:, m, P * k:P * k + P], bmat[:, m],
                                  start=(m == 0), stop=(m == NG - 1))
                pe.wait_ge(consts_dve, 5)
                pe.wait_ge(consts_pool, 5)
                pe.matmul(bank[3][0:PR, 1, 0:B], prob_part[:], sel_batch[:], start=True, stop=True)\
                    .then_inc(set_t, 1)
                pe.wait_ge(set_e, 8)
                for k in range(NG):
                    pe.matmul(unit[1][S:P, 0, 0:1], wu_raw[:, k], vecs[:, 3, k:k + 1], start=(k == 0), stop=False)
                for m in range(NG):
                    last = pe.matmul(unit[1][S:P, 0, 0:1], bmat[:, m], vecs[:, 4, m:m + 1],
                                     start=False, stop=(m == NG - 1))
                last.then_inc(set_t, 1)
                pe.matmul(bank[2][0:B, 0, :], prob_meanT[:], wprogT, start=True, stop=True).then_inc(set_t, 1)
                for k in range(NG):
                    last = pe.matmul(unit[1][:, 2], bv[:, k:k + 1].broadcast_to([P, P]), woT[:, k],
                                     start=(k == 0), stop=(k == NG - 1))
                last.then_inc(set_t, 1)
                pe.wait_ge(set_e, 12)
                pe.wait_ge(consts_pool, 9)

            def transposes(src, other, dst):
                for c in range(NC):
                    for k in range(NG):
                        last = pe.transpose(dst[:, k, P * c:P * c + P], src[:, other, c, P * k:P * k + P], ident[:])
                return last

            def product3(bnk, left, right, low_ready, value):
                for n, (a, w) in enumerate(((0, 0), (0, 1), (1, 0))):
                    if a:
                        wait(pe, low_ready, value)
                    for m in range(2):
                        for k in range(NG):
                            last = pe.matmul(bnk[:, m], left(a, w, k, m), right(a, w, k),
                                             start=(n == 0 and m == 0 and k == 0),
                                             stop=(n == 2 and m == 1 and k == NG - 1))
                return last

            def project(n, bnk, src, low_ready, value):
                return product3(bnk, lambda a, w, k, g: (wT_lo if w else wT_hi)[:, k, H * n + P * g:H * n + P * g + P],
                                lambda a, w, k: src[a][:, k], low_ready, value)

            def project_v(low_ready, value):
                return product3(bank_c, lambda a, w, k, c: (cnT_lo if a else cnT_hi)[:, k, P * c:P * c + P],
                                lambda a, w, k: (wT_lo if w else wT_hi)[:, k, 2 * H:3 * H], low_ready, value)

            def one_slot(s, pair, parity):
                other = 1 - parity

                def scores(b, parity, n):
                    g, c = divmod(n, 2)
                    if n < 2:
                        wait(pe, exp_done, 4 * b - 1 + n)
                    else:
                        wait(pe, max_done, 4 * b + n - 1)
                    for j in range(NJ):
                        last = pe.matmul(unit[n % 2][:, j], q_stack[parity][:, j, g, P * c:P * c + P],
                                         k_stack[parity][:, j, g], start=True, stop=True)
                    last.then_inc(score_psum, 1)

                def maxima(c, done):
                    wait(pe, max_done, 4 * s + 3 + c)
                    pe.transpose(unit[c][0:MR + NH, 0, P * c:P * c + P], neg_max[:, c], ident[:]).then_inc(done, 1)

                def logits(n):
                    g, c = divmod(n, 2)
                    if n == 0:
                        wait(pe, maxT0_done, s + 1)
                        wait(pe, maxT1_done, s + 1)
                    elif n > 1:
                        wait(pe, exp_done, 4 * s + n - 1)
                    for j in range(NJ):
                        last = pe.matmul(unit[n % 2][:, j], k_stack[parity][:, j, g, P * c:P * c + P],
                                         q_stack[parity][:, j, g], start=True, stop=True)
                    last.then_inc(logit_psum, 1)

                def values(n):
                    g, c = divmod(n, 2)
                    wait(pe, exp_done, 4 * s + n + 1)
                    if n == 0:
                        wait(pe, v_done, s + 1)
                        wait(pe, oT_done, 2 * s)
                        wait(pe, u_done, s - 1)
                    for m in range(2):
                        for j in range(NJ):
                            h = NJ * g + j
                            w = ones_hd[:] if m else v_sb[:, parity, c, HD * h:HD * h + HD]
                            last = pe.matmul(bank_o[g][HD * j:HD * j + HD, m], w, probs_exp[n % 2][:, j],
                                             start=(c == 0 and m == 0), stop=(c == NC - 1 and m == 1),
                                             tile_position=(0, HD * j))
                    last.then_inc(pv_psum, 1)

                if has(s, 1):
                    wait(pe, norm1_done, s + 2)
                    wait(pe, k_done, s + 1)
                    wait(pe, x2T_done, s - 1)
                    transposes(xn, other, bank_x).then_inc(xT_psum, 1)
                if has(s, -2):
                    wait(pe, x2T_done, s - 1)
                    wait(pe, oT_done, 2 * s - 1 if has(s, -1) else 2 * B)
                    for k in range(NG):
                        last = pe.matmul(bank_o[0][S:P, 0, :], wu[:, k], xn2T[:, k], start=(k == 0), stop=(k == NG - 1))
                    last.then_inc(u_psum, 1)
                if has(s, 1):
                    wait(pe, v_done, s + 1)
                    wait(pe, x1_done, s - 1)
                    transposes(cn, other, bank_c).then_inc(cT_psum, 1)
                if has(s, 0):
                    scores(s, parity, 2)
                if has(s, 1):
                    wait(pe, xT_done, s + 2)
                    project(0, bank_x, (xnT_hi, xnT_lo), x_split, s + 2).then_inc(q_psum, 1)
                if has(s, 0):
                    scores(s, parity, 3)
                    maxima(0, maxT0_psum)
                if has(s, 1):
                    wait(pe, cT_done, s + 2)
                    project_v(c_split, s + 2).then_inc(v_psum, 1)
                if has(s, 0):
                    maxima(1, maxT1_psum)
                if has(s, 1):
                    wait(pe, q_done, s + 2)
                    project(1, bank_x, (cnT_hi, cnT_lo), c_split, s + 2).then_inc(k_psum, 1)
                if has(s, 0):
                    logits(0)
                    logits(1)
                if has(s, -1):
                    wait(pe, oT_done, 2 * s)
                    if has(s, 1):
                        wait(pe, v_done, s + 2)
                    else:
                        wait(pe, x1_done, s - 1)
                    for c in range(NC):
                        for g in range(NG):
                            last = pe.matmul(bank_c[:, c], oT[:, g, P * c:P * c + P], woT[:, g],
                                             start=(g == 0), stop=(g == NG - 1))
                    last.then_inc(y_psum, 1)
                if has(s, 0):
                    values(0)
                    logits(2)
                    values(1)
                    logits(3)
                    values(2)
                    values(3)
                if has(s, -1):
                    wait(pe, norm2_done, s)
                    if has(s, 1):
                        wait(pe, k_done, s + 2)
                    else:
                        wait(pe, x2T_done, s - 1)
                    for c in range(NC):
                        for k in range(NG):
                            last = pe.transpose(bank_x[:, k, P * c:P * c + P], xn2[:, c, P * k:P * k + P], ident[:])
                    last.then_inc(x2T_psum, 1)
                if isinstance(s, int) and s == -1:
                    setup_rest()
                if has(s, 1):
                    wait(pe, stack_in[other], STACK * (pair + parity + 1))
                    scores(s + 1, other, 0)
                    scores(s + 1, other, 1)

            slots(pe, one_slot)

            def output(c, k, n):
                q, g = NK * c + k, n // GB
                if n == 0:
                    pe.wait_ge(stage_done, q + 1)
                if n % GB == 0:
                    pe.wait_ge(out_done[g], q + 1)
                prod = pe.matmul(unit[g][TO * (c % 2):TO * (c % 2) + TO, n % GB], yu_stage[:, n], c2[:],
                                 start=True, stop=True)
                if n % GB == GB - 1:
                    prod.then_inc(out_psum, 1)

            for c in range(T // TO):
                with pe.Fori(0, NK // 2) as i:
                    for h in range(2):
                        k = 2 * i + h
                        pe.wait_ge(u_loaded, NK * c + k + 1)
                        for j in range(BS):
                            pe.wait_ge(y_ready, TO * c + BS * k + j + 1)
                            pe.matmul(bank[j % 2][0:S, 0, 0:B], aT2[:], ring[:, (BS * h + j - 1) % (2 * BS), :],
                                      start=True, stop=True).then_inc(z_ready, 1)
                            if c > 0 and j >= BS - 2 * GB:
                                output(c - 1, k, j - (BS - 2 * GB))
            with pe.Fori(0, NK) as k:
                for n in range(2 * GB):
                    output(T // TO - 1, k, n)


_INS = ["x", "ctx_1024", "itok_BxS2_4_31999", "ctxb_2048x64", "L0_xattn_A", "L0_xattn_Bmat", "L0_xattn_Cmat",
        "L0_xattn_W_in", "L0_xattn_b_in", "L0_xattn_W_qkv", "L0_xattn_b_qkv", "L0_xattn_W_o", "L0_xattn_b_o",
        "L0_xattn_W_prog", "L0_xattn_b_prog", "L0_xattn_g1", "L0_xattn_beta1", "L0_xattn_g2", "L0_xattn_beta2"]


def kernel(**inputs):
    import numpy as np
    import concourse.bacc as bacc
    from concourse import mybir as mb
    from concourse.bass_utils import run_bass_kernel_spmd

    nc = bacc.Bacc("TRN2", target_bir_lowering=False, num_devices=1)
    arrays, args = {}, []
    for name in _INS:
        a = np.ascontiguousarray(inputs[name])
        arrays[f"in_{name}"] = a
        args.append(nc.dram_tensor(f"in_{name}", a.shape, mb.dt.from_np(a.dtype), kind="ExternalInput").ap())
    out = nc.dram_tensor("out_0", inputs["x"].shape, mb.dt.float32, kind="ExternalOutput").ap()
    xattn_seq_kernel(nc, *args, out)
    result = run_bass_kernel_spmd(nc, [arrays], core_ids=[0])
    return result.results[0]["out_0"]
```
